# Optimizing a Trainium2 kernel written in Bass

```python
import numpy as np
import jax
import jax.numpy as jnp

def _softmax(x, axis=-1):
    return jax.nn.softmax(x, axis=axis)

def _gelu(x):
    return jax.nn.gelu(x, approximate=True)

def _silu(x):
    return jax.nn.silu(x)

def _sigmoid(x):
    return jax.nn.sigmoid(x)

def _layernorm(x, axis=-1, eps=1e-05):
    m = jnp.mean(x, axis=axis, keepdims=True)
    v = jnp.var(x, axis=axis, keepdims=True)
    return (x - m) / jnp.sqrt(v + eps)

def _scatter_add(tgt, idx, src, axis=0):
    return tgt.at[idx].add(src)

def _segment_sum(src, seg, n):
    return jax.ops.segment_sum(src, seg, n)
kernel_name = 'mk_conv_preact_d2_conv_nchw32_r2_99e93e'

def setup_inputs(seed: int=0):
    np.random.seed(seed)
    _w = jnp.asarray

    def _rec_inputs():
        import jax
        import jax.numpy as jnp
        _gk = jax.random.key(seed)
        x = -0.000125 + 0.9999 * jax.random.normal(jax.random.fold_in(_gk, 1), (16, 32, 128, 128), jnp.float32)
        return x
    x = _rec_inputs()

    def _L0_conv_setup():
        import jax, jax.numpy as jnp
        import numpy as np
        STRIDE = 1
        PADDING = 1
        key = jax.random.key(seed)
        k1, k2 = jax.random.split(key)
        x = jax.random.normal(k1, (16, 32, 128, 128), dtype=jnp.float32)
        weight = jax.random.normal(k2, (32, 32, 3, 3), dtype=jnp.float32) * 0.05
        threshold = jnp.array([0.04], dtype=jnp.float32)
        return {'x': x, 'weight': weight, 'threshold': threshold}
    _L0_conv_all = _L0_conv_setup()
    _L0_conv_in = {k: v for k, v in _L0_conv_all.items() if k in ('weight', 'threshold')}
    del _L0_conv_all

    def _L1_conv_setup():
        import jax, jax.numpy as jnp
        import numpy as np
        BS, CIN, COUT, H, W, K = (16, 32, 32, 112, 112, 5)
        key = jax.random.key(seed)
        k1, k2 = jax.random.split(key)
        img = jax.random.normal(k1, (BS, CIN, H, W), dtype=jnp.float32)
        kernel = jax.random.uniform(k2, (COUT, CIN, K, K), dtype=jnp.float32, minval=-0.1, maxval=0.1)
        bias = jnp.zeros((COUT,), dtype=jnp.float32)
        return {'img': img, 'kernel': kernel, 'bias': bias}
    _L1_conv_all = _L1_conv_setup()
    _L1_conv_in = {k: v for k, v in _L1_conv_all.items() if k in ('kernel', 'bias')}
    del _L1_conv_all
    return {'x': x, 'L0_conv_weight': _L0_conv_in['weight'], 'L0_conv_threshold': _L0_conv_in['threshold'], 'L1_conv_kernel': _L1_conv_in['kernel'], 'L1_conv_bias': _L1_conv_in['bias']}

def reference(x, L0_conv_weight, L0_conv_threshold, L1_conv_kernel, L1_conv_bias):
    import jax
    import jax.numpy as jnp

    def _L0_conv_ref(x, weight, threshold):
        import jax, jax.numpy as jnp
        import numpy as np
        STRIDE = 1
        PADDING = 1
        out_c = weight.shape[0]
        thr = jnp.maximum(threshold, 0.0)
        score = jnp.sum(jnp.abs(weight), axis=0) / float(out_c)
        mask = (score - thr > 0.0).astype(weight.dtype)
        ratio = jnp.sum(mask) / mask.size
        mask0 = (score > 0.0).astype(weight.dtype)
        mask = jnp.where(ratio <= 0.01, mask0, mask)
        w_masked = weight * mask[None, :, :, :]
        out = jax.lax.conv_general_dilated(x, w_masked, window_strides=(STRIDE, STRIDE), padding=((PADDING, PADDING), (PADDING, PADDING)), dimension_numbers=('NCHW', 'OIHW', 'NCHW'))
        return out

    def _L1_conv_ref(img, kernel, bias):
        import jax, jax.numpy as jnp
        import numpy as np
        BS, CIN, COUT, H, W, K = (16, 32, 32, 112, 112, 5)
        out_c, in_c, k, _ = kernel.shape
        bs, _, h, w = img.shape
        new_h, new_w = (h + k - 1, w + k - 1)
        pad = (k - 1) // 2
        pimg = jnp.pad(img, ((0, 0), (0, 0), (pad, pad), (pad, pad)))
        kc = k // 2
        idx = np.arange(k)
        kny = (k - 1 - idx - kc) % new_h
        knx = (k - 1 - idx - kc) % new_w
        pkernel = jnp.zeros((out_c, in_c, new_h, new_w), img.dtype)
        pkernel = pkernel.at[:, :, kny[:, None], knx[None, :]].set(kernel)
        X = jnp.fft.fft2(pimg)
        Kf = jnp.fft.fft2(pkernel)
        Y = jnp.einsum('bihw,oihw->bohw', X, Kf)
        y = jnp.fft.ifft2(Y).real
        return y[:, :, pad:new_h - pad, pad:new_w - pad] + bias[None, :, None, None]

    def _gn(v, G=16, eps=1e-05):
        B_, C_, H_, W_ = v.shape
        g = v.reshape(B_, G, C_ // G, H_, W_)
        m = jnp.mean(g, axis=(2, 3, 4), keepdims=True)
        s = jnp.var(g, axis=(2, 3, 4), keepdims=True)
        return ((g - m) / jnp.sqrt(s + eps)).reshape(v.shape)

    def _ln_c(v, eps=1e-06):
        m = jnp.mean(v, axis=1, keepdims=True)
        s = jnp.var(v, axis=1, keepdims=True)
        return (v - m) / jnp.sqrt(s + eps)

    def _ln_t(v, eps=1e-05):
        m = jnp.mean(v, axis=-1, keepdims=True)
        s = jnp.var(v, axis=-1, keepdims=True)
        return (v - m) / jnp.sqrt(s + eps)

    def _to_tokens(v):
        B_, C_, H_, W_ = v.shape
        return v.reshape(B_, C_, H_ * W_).transpose(0, 2, 1)

    def _from_tokens(t, like):
        B_, C_, H_, W_ = like.shape
        return t.transpose(0, 2, 1).reshape(B_, C_, H_, W_)
    x = x + _L0_conv_ref(_gn(x), L0_conv_weight, L0_conv_threshold)
    x = x + _L1_conv_ref(_gn(x), L1_conv_kernel, L1_conv_bias)
    return x

_drawn_inputs = setup_inputs


def setup_inputs(seed=0):
    import zlib

    import numpy as np

    out = dict(_drawn_inputs(seed))
    spreads = {'L1_conv_bias': (0.0, 0.1)}
    factors = {}
    for name, (base, spread) in spreads.items():
        noise = np.random.default_rng([zlib.crc32(name.encode()), seed]).standard_normal(out[name].shape)
        drawn = base * np.exp(spread * noise) if base else spread * noise
        out[name] = jnp.asarray(drawn.astype(out[name].dtype))
    for name, factor in factors.items():
        out[name] = (out[name] * factor).astype(out[name].dtype)
    return out
```

```python
from contextlib import ExitStack

import concourse.bass as bass
import concourse.mybir as mybir

F32 = mybir.dt.float32
F16 = mybir.dt.float16
U32 = mybir.dt.uint32
ALU = mybir.AluOpType
ACT = mybir.ActivationFunctionType
AX = mybir.AxisListType

C = 32
Q = 4
P = Q * C
K3, K5 = 3, 5
GROUP = 2
EPS = 1e-5
SLOTS = 8
BANKS = 4
B_MEAN, B_VAR, B_SETUP = 4, 5, 6
PIX = 2.0 ** 7
LOW = 2.0 ** 11
WTOP = 2.0 ** 14


class Image:

    def __init__(self, k, c):
        self.k, self.c = k, c

    def __add__(self, d):
        return Image(self.k, self.c + d)

    def number(self):
        return self.c if isinstance(self.k, int) and self.k == 0 else 2 * self.k + self.c

    def buffer(self):
        return self.c % 2

    def uses(self):
        return self.k + self.c // 2


def two_blocks(nc, x, w3_dram, thr_dram, w5_dram, bias_dram, mix_dram, out):
    N, _, H, W = x.shape
    NJ = H // Q
    JS = NJ // SLOTS
    PITCH = W + 4
    T3, T5 = K3 * K3, K5 * K5

    with ExitStack() as ctx:
        def sbuf(name, shape, dt=F32):
            return ctx.enter_context(nc.sbuf_tensor(name, shape, dt))

        def sem(name):
            return ctx.enter_context(nc.semaphore(name))

        x_odd = sbuf("x_odd", [P, NJ + 1, W])
        x_even = sbuf("x_even", [P, 2, NJ, W])
        mid = sbuf("mid", [P, 2, NJ, W])
        conv_out = sbuf("conv_out", [P, BANKS, JS, W])
        a_hi = sbuf("a_hi", [P, NJ + 1, PITCH], F16)
        a_lo = sbuf("a_lo", [P, NJ + 1, PITCH], F16)
        b_hi = sbuf("b_hi", [P, NJ, PITCH], F16)
        b_lo = sbuf("b_lo", [P, NJ, PITCH], F16)
        m_hi = sbuf("m_hi", [P, NJ + 2, PITCH], F16)
        pairs = sbuf("pairs", [P, NJ + 1, 2, PITCH], F16)
        norm = sbuf("norm", [P, 2, JS, W])
        m_lo = sbuf("m_lo", [P, 2, JS, W], F16)
        mix = sbuf("mix", [P, P])
        bn = sbuf("bn", [P, 2, SLOTS, 6])
        mv = sbuf("mv", [P, 2, 2])
        gmean = sbuf("gmean", [P, 2])
        spread = sbuf("spread", [P, 2])
        gvar = sbuf("gvar", [P, 2])
        root = sbuf("root", [P, 2])
        rinv = sbuf("rinv", [P, 2])
        newton = sbuf("newton", [P, 2])
        gscale = sbuf("gscale", [P, 2])
        zrow = sbuf("zrow", [C, W])
        carrier = sbuf("carrier", [P, 2])
        w3 = sbuf("w3", [P, C, T3])
        w5 = sbuf("w5", [P, C, T5])
        w3n = sbuf("w3n", [P, C, T3])
        parts3 = [sbuf(f"w3_{n}", [P, C, T3], F16) for n in ("hi", "his", "lo")]
        parts5 = [sbuf(f"w5_{n}", [P, C, T5], F16) for n in ("hi", "his", "lo")]
        thr = sbuf("thr", [P, 1])
        bias = sbuf("bias", [P, 1])
        ones = sbuf("ones", [P, P])
        score = sbuf("score", [P, T3])
        mask = sbuf("mask", [P, T3])
        mask0 = sbuf("mask0", [P, T3])
        small = sbuf("small", [P, 8])
        bound = sbuf("bound", [P, 2])
        power = sbuf("power", [P, 2])
        wfac = sbuf("wfac", [P, 2])
        unscale = sbuf("unscale", [P, 2])
        s3 = sbuf("s3", [P, 3, K3, 2 * C], F16)
        s5_pair = sbuf("s5_pair", [P, 3, K5, 2 * C], F16)
        s5_low = sbuf("s5_low", [P, 2, 2, K5, 2 * C], F16)
        psum = ctx.enter_context(nc.psum_tensor("psum", [P, 8, 512], F32))

        w_loaded = sem("w_loaded")
        wstep = sem("wstep")
        wchain = sem("wchain")
        ones_set = sem("ones_set")
        zeroed = sem("zeroed")
        w_summed = sem("w_summed")
        w3_split = sem("w3_split")
        w5_split = sem("w5_split")
        s3_set = sem("s3_set")
        placed = sem("placed")
        odd_in = sem("odd_in")
        even_in = [sem("even_in0"), sem("even_in1")]
        stored = [sem("stored0"), sem("stored1")]
        c1_done = sem("c1_done")
        c1_read = sem("c1_read")
        c2_done = sem("c2_done")
        c2_read = sem("c2_read")
        out_added = sem("out_added")
        bn_x = sem("bn_x")
        bn_mid = sem("bn_mid")
        stat_ready = sem("stat_ready")
        mean_mixed = sem("mean_mixed")
        spread_ready = sem("spread_ready")
        var_mixed = sem("var_mixed")
        var_ready = sem("var_ready")
        root_ready = sem("root_ready")
        gstep = sem("gstep")
        pad_set = sem("pad_set")
        norm1 = sem("norm1")
        hi1 = sem("hi1")
        lo1 = sem("lo1")
        ready1 = sem("ready1")
        norm2 = sem("norm2")
        hi2 = sem("hi2")
        lo2 = sem("lo2")
        ready2 = sem("ready2")

        RUN1 = NJ // 4
        ITEMS1 = 5
        ITEMS2 = SLOTS
        PLAN = {2: [(1, 0), (2, 0), (2, 1)], 3: [(1, 1), (2, 2)], 4: [(1, 2), (2, 3)],
                5: [(1, 3), (2, 4)], 6: [(1, 4), (2, 5)], 7: [(2, 6), (2, 7)]}

        def plan(i_first, i_last):
            return {s: [t for t in ts if not (t[0] == 2 and i_first) and not (t[0] == 1 and i_last)]
                    for s, ts in PLAN.items()}

        STEPS_G = 8

        def turns(eng, turn):
            turn(Image(0, -1), first=True)
            turn(Image(0, 0))
            turn(Image(0, 1), inner=True)
            turn(Image(0, 2), inner=True)
            with eng.Fori(0, (N - 4) // 2) as k:
                turn(Image(k, 3), inner=True)
                turn(Image(k, 4), inner=True)
            turn(Image(0, N - 1), last=True)
            turn(Image(0, N), end=True)

        def rows(image, r):
            return image.rearrange("c (j q) w -> q c j w", q=Q)[r]

        block = ctx.enter_context(nc.Block())

        @block.sync
        def _(sp):
            for q in range(Q):
                part = slice(q * C, (q + 1) * C)
                sp.dma_start(w3[part, :, :], w3_dram.rearrange("o i a b -> i o (a b)")).then_inc(w_loaded, 16)
                sp.dma_start(w5[part, :, :], w5_dram.rearrange("o i a b -> i o (a b)")).then_inc(w_loaded, 16)
                sp.dma_start(bias[part, :], bias_dram.rearrange("(o a) -> o a", a=1)).then_inc(w_loaded, 16)
            sp.dma_start(thr[:, :], thr_dram.rearrange("(a o) -> a o", a=1).to_broadcast([P, 1])).then_inc(w_loaded, 16)
            sp.dma_start(mix[:, :], mix_dram).then_inc(w_loaded, 16)

            def load_even(im):
                for q in range(Q):
                    nc.sync.dma_start(x_even[q * C:(q + 1) * C, im.buffer(), :, :],
                                      rows(x[im.number()], q)).then_inc(even_in[im.buffer()], 16)

            def load_odd(im):
                for q in range(Q):
                    first = 1 if q == 0 else 0
                    nc.sync.dma_start(x_odd[q * C:(q + 1) * C, first:first + NJ, :],
                                      rows(x[im.number()], (q + 3) % Q)).then_inc(odd_in, 16)

            def turn(i, first=False, inner=False, last=False, end=False):
                if first:
                    load_even(i + 1)
                    load_odd(i + 1)
                    load_even(i + 2)
                    return
                if not (last or end):
                    sp.wait_ge(lo1, ITEMS1 * (i.number() + 1))
                    load_odd(i + 1)
                    sp.wait_ge(c1_read, SLOTS * (i.number() + 1))
                    if not isinstance(i.k, int) or i.number() < N - 2:
                        load_even(i + 2)
                if inner or last or end:
                    o = i + -1
                    for s in range(0, SLOTS, 2):
                        sp.wait_ge(out_added, SLOTS * o.number() + s + 2)
                        for q in range(Q):
                            nc.sync.dma_start(
                                rows(out[o.number()], q)[:, s * JS:(s + 2) * JS, :],
                                mid[q * C:(q + 1) * C, o.buffer(), s * JS:(s + 2) * JS, :],
                            ).then_inc(stored[o.buffer()], 16)

            turn(Image(0, -1), first=True)
            turn(Image(0, 0))
            turn(Image(0, 1), inner=True)
            turn(Image(0, 2), inner=True)
            with sp.Fori(0, (N - 6) // 2) as k:
                turn(Image(k, 3), inner=True)
                turn(Image(k, 4), inner=True)
            turn(Image(0, N - 3), inner=True)
            turn(Image(0, N - 2), inner=True)
            turn(Image(0, N - 1), last=True)
            turn(Image(0, N), end=True)
            for b in range(2):
                sp.wait_ge(stored[b], 16 * Q * (SLOTS // 2) * (N // 2))

        @block.gpsimd
        def _(pool):
            nc.gpsimd.memset(zrow[:, :], 0.0)
            for t in (a_hi, a_lo, b_hi, b_lo, m_hi):
                nc.gpsimd.memset(t[:, :, 0:2], 0.0)
                nc.gpsimd.memset(t[:, :, PITCH - 2:PITCH], 0.0)
            nc.gpsimd.memset(pairs[:, :, :, 0:2], 0.0)
            nc.gpsimd.memset(pairs[:, :, :, PITCH - 2:PITCH], 0.0)
            nc.gpsimd.memset(m_hi[:, 0, 2:2 + W], 0.0)
            nc.gpsimd.memset(m_hi[:, NJ + 1, 2:2 + W], 0.0)
            nc.gpsimd.memset(pairs[:, 0, 0, 2:2 + W], 0.0)
            nc.gpsimd.memset(pairs[:, NJ, 1, 2:2 + W], 0.0)
            nc.gpsimd.memset(s5_pair[:, :, :, :], 0.0)
            nc.gpsimd.memset(s5_low[:, :, :, :, :], 0.0).then_inc(zeroed, 1)

            pool.wait_ge(w5_split, 3)
            pool.wait_ge(zeroed, 1)
            hi, his, lo = parts5
            copies = [0]

            def place(dst, src):
                nc.gpsimd.tensor_copy(dst, src).then_inc(placed, 1)
                copies[0] += 1
                pool.wait_ge(placed, copies[0])

            def taps(t, part, dy):
                return t[part, :, dy * K5:(dy + 1) * K5].rearrange("p o t -> p t o")

            for d in range(-1, 2):
                for r in range(2):
                    for o in range(2):
                        dy = 2 * d + r - o + K5 // 2
                        if 0 <= dy < K5:
                            for half, t in ((0, hi), (2, his)):
                                part = slice((half + r) * C, (half + r + 1) * C)
                                place(s5_pair[part, d + 1, :, o * C:(o + 1) * C], taps(t, part, dy))
            for t in range(2):
                for off in range(2):
                    for q in range(Q):
                        for o in range(2):
                            dy = Q * (off + t - 1) + q - 2 * t - o + K5 // 2
                            if 0 <= dy < K5:
                                part = slice(q * C, (q + 1) * C)
                                place(s5_low[part, t, off, :, o * C:(o + 1) * C], taps(lo, part, dy))

            def turn(o):
                for s in range(SLOTS):
                    pool.wait_ge(c2_read, SLOTS * o.number() + s + 1)
                    m = mid[:, o.buffer(), s * JS:(s + 1) * JS, :]
                    nc.gpsimd.tensor_tensor(m, m, conv_out[:, s % BANKS, :, :], ALU.add).then_inc(out_added, 1)

            with pool.Fori(0, N // 2) as k:
                turn(Image(k, 0))
                turn(Image(k, 1))

        @block.scalar
        def _(act):
            def high(which, j, i):
                if which == 1:
                    n = i + 1
                    act.wait_ge(norm1, ITEMS1 * n.number() + j + 1)
                    if j < 4:
                        src = x_odd[:, j * RUN1:(j + 1) * RUN1, :]
                        dst = a_hi[:, j * RUN1:(j + 1) * RUN1, 2:2 + W]
                    else:
                        src = x_odd[0:C, NJ, :]
                        dst = a_hi[0:C, NJ, 2:2 + W]
                    nc.scalar.activation(dst, src, ACT.Copy, scale=1.0 / LOW).then_inc(hi1, 1)
                else:
                    act.wait_ge(norm2, ITEMS2 * i.number() + j + 1)
                    nc.scalar.activation(m_hi[:, 1 + j * JS:1 + (j + 1) * JS, 2:2 + W], norm[:, j % 2, :, :],
                                         ACT.Copy, scale=1.0 / LOW).then_inc(hi2, 1)

            def turn(i, first=False, inner=False, last=False, end=False):
                o = i + -1
                steps = plan(first, last)
                for s in range(SLOTS):
                    if inner or last or end:
                        act.wait_ge(c2_done, SLOTS * o.number() + s + 1)
                        if s >= BANKS or not (isinstance(o.k, int) and o.number() == 0):
                            act.wait_ge(out_added, SLOTS * o.number() + s + 1 - BANKS)
                        nc.scalar.activation(conv_out[:, s % BANKS, :, :],
                                             psum[:, s % BANKS, :].rearrange("p (j w) -> p j w", j=JS),
                                             ACT.Identity, bias=bias[:, 0:1], scale=unscale[:, 1:2]).then_inc(c2_read, 1)
                    if end:
                        continue
                    if s == 2:
                        act.wait_ge(var_ready, i.number() + 2)
                        c0, c1 = (0, 1) if first else (1, 2) if last else (0, 2)
                        nc.scalar.activation(root[:, c0:c1], gvar[:, c0:c1], ACT.Sqrt).then_inc(root_ready, 1)
                    for which, j in steps.get(s, []):
                        high(which, j, i)

            act.wait_ge(wstep, 1)
            turns(act, turn)

        @block.vector
        def _(dve):
            nc.vector.memset(ones[:, :], 1.0).then_inc(ones_set, 1)
            nc.vector.memset(s3[:, :, :, :], 0.0)
            for t in (a_hi, a_lo):
                nc.vector.memset(t[C:2 * C, NJ, 2:2 + W], 0.0)
            steps_w = [0]

            def own_step(ins):
                steps_w[0] += 1
                ins.then_inc(wchain, 1)
                dve.wait_ge(wchain, steps_w[0])

            dve.wait_ge(w_loaded, 16 * 14)
            own_step(nc.vector.tensor_reduce(score[:, :], w3[:, :, :].rearrange("p o t -> p t o"), AX.X, ALU.add,
                                             apply_absolute_value=True))
            own_step(nc.vector.tensor_scalar(small[:, 0:1], thr[:, :], 0.0, None, ALU.max))
            own_step(nc.vector.tensor_scalar(mask[:, :], score[:, :], 1.0 / C, small[:, 0:1], ALU.mult, ALU.subtract))
            own_step(nc.vector.tensor_scalar(mask[:, :], mask[:, :], 0.0, None, ALU.is_gt))
            own_step(nc.vector.tensor_scalar(mask0[:, :], score[:, :], 1.0 / C, 0.0, ALU.mult, ALU.is_gt))
            own_step(nc.vector.tensor_reduce(small[:, 1:2], mask[:, :], AX.X, ALU.add))
            dve.wait_ge(w_summed, 1)
            own_step(nc.vector.tensor_scalar(small[:, 2:3], psum[:, B_SETUP, 0:1], 1.0 / (Q * C * T3), 0.01,
                                             ALU.mult, ALU.is_le))
            own_step(nc.vector.scalar_tensor_tensor(mask[:, :], mask0[:, :], small[:, 2:3], mask[:, :], ALU.mult, ALU.max))
            for t in range(T3):
                own_step(nc.vector.tensor_scalar(w3n[:, :, t], w3[:, :, t], mask[:, t:t + 1], None, ALU.mult))
            own_step(nc.vector.tensor_reduce(bound[:, 0:1], w3n[:, :, :].rearrange("p o t -> p (o t)"), AX.X, ALU.max,
                                             apply_absolute_value=True))
            own_step(nc.vector.tensor_reduce(bound[:, 1:2], w5[:, :, :].rearrange("p o t -> p (o t)"), AX.X, ALU.max,
                                             apply_absolute_value=True))
            dve.wait_ge(w_summed, 2)
            own_step(nc.vector.tensor_scalar(power[:, :], psum[:, B_SETUP, 8:10], 2.0 ** -100, None, ALU.max))
            own_step(nc.vector.tensor_scalar(power[:, :].bitcast(U32), power[:, :].bitcast(U32), 0x7F800000, None,
                                             ALU.bitwise_and))
            own_step(nc.vector.reciprocal(wfac[:, :], power[:, :]))
            own_step(nc.vector.tensor_scalar(wfac[:, :], wfac[:, :], WTOP, None, ALU.mult))
            own_step(nc.vector.tensor_scalar(unscale[:, :], power[:, :], 1.0 / (WTOP * PIX), None, ALU.mult))
            for w, n, (hi, his, lo), split in ((w3n, 0, parts3, w3_split), (w5, 1, parts5, w5_split)):
                own_step(nc.vector.tensor_scalar(w[:, :, :], w[:, :, :], wfac[:, n:n + 1], None, ALU.mult))
                own_step(nc.vector.tensor_copy(hi[:, :, :], w[:, :, :]))
                nc.vector.tensor_scalar(his[:, :, :], hi[:, :, :], 1.0 / LOW, None, ALU.mult).then_inc(split, 1)
                nc.vector.tensor_tensor(lo[:, :, :], w[:, :, :], hi[:, :, :], ALU.subtract).then_inc(split, 2)
            dve.wait_ge(w3_split, 3)
            for n, t in enumerate(parts3):
                for q in range(Q):
                    for o in range(2):
                        if 0 <= q - o < K3:
                            part = slice(q * C, (q + 1) * C)
                            last = nc.vector.tensor_copy(
                                s3[part, n, :, o * C:(o + 1) * C],
                                t[part, :, (q - o) * K3:(q - o + 1) * K3].rearrange("p o t -> p t o"))
            last.then_inc(s3_set, 1)
            dve.wait_ge(s3_set, 1)
            nc.vector.memset(small[:, 3:4], 0.0).then_inc(wstep, 1)
            dve.wait_ge(zeroed, 1)

            def normalize(which, j, i):
                if which == 1:
                    if j < 4:
                        v = x_odd[:, j * RUN1:(j + 1) * RUN1, :]
                        m, s = gmean[:, 0:1], gscale[:, 0:1]
                    else:
                        v = x_odd[0:C, NJ, :]
                        m, s = gmean[0:C, 0:1], gscale[0:C, 0:1]
                    nc.vector.tensor_scalar(v, v, m, s, ALU.subtract, ALU.mult).then_inc(norm1, 1)
                else:
                    if j >= 2:
                        dve.wait_ge(hi2, ITEMS2 * i.number() + j - 1)
                    nc.vector.tensor_scalar(norm[:, j % 2, :, :], mid[:, i.buffer(), j * JS:(j + 1) * JS, :],
                                            gmean[:, 1:2], gscale[:, 1:2], ALU.subtract, ALU.mult).then_inc(norm2, 1)

            def low(which, j, i):
                if which == 1:
                    n = i + 1
                    count = ITEMS1 * n.number() + j + 1
                    dve.wait_ge(hi1, count)
                    if j < 4:
                        part, b0, b1 = slice(0, P), j * RUN1, (j + 1) * RUN1
                    else:
                        part, b0, b1 = slice(0, C), NJ, NJ + 1
                    nc.vector.scalar_tensor_tensor(a_lo[part, b0:b1, 2:2 + W], a_hi[part, b0:b1, 2:2 + W], -LOW,
                                                   x_odd[part, b0:b1, :], ALU.mult, ALU.add).then_inc(lo1, 1)
                    dve.wait_ge(lo1, count)
                    for a, b in ((a_hi, b_hi), (a_lo, b_lo)):
                        if j < 4:
                            nc.vector.tensor_copy(b[0:2 * C, b0:b1, 2:2 + W], a[2 * C:P, b0:b1, 2:2 + W])
                        first = max(b0, 1)
                        last = nc.vector.tensor_copy(b[2 * C:P, first - 1:b1 - 1, 2:2 + W],
                                                     a[0:2 * C, first:b1, 2:2 + W])
                    last.then_inc(ready1, 1)
                else:
                    count = ITEMS2 * i.number() + j + 1
                    dve.wait_ge(hi2, count)
                    nc.vector.scalar_tensor_tensor(m_lo[:, j % 2, :, :], m_hi[:, 1 + j * JS:1 + (j + 1) * JS, 2:2 + W],
                                                   -LOW, norm[:, j % 2, :, :], ALU.mult, ALU.add).then_inc(lo2, 1)
                    dve.wait_ge(lo2, count)
                    for t in range(2):
                        dst = pairs[:, j * JS + t:(j + 1) * JS + t, 1 - t, 2:2 + W]
                        src = slice(2 * C * t, 2 * C * (t + 1))
                        nc.vector.tensor_copy(dst[0:2 * C], m_hi[src, 1 + j * JS:1 + (j + 1) * JS, 2:2 + W])
                        last = nc.vector.tensor_copy(dst[2 * C:P], m_lo[src, j % 2, :, :])
                    last.then_inc(ready2, 1)

            def turn(i, first=False, inner=False, last=False, end=False):
                if end:
                    return
                def stats_mid(s):
                    dve.wait_ge(c1_read, SLOTS * i.number() + s + 1)
                    nc.vector.bn_stats(bn[:, 1, s, :], mid[:, i.buffer(), s * JS:(s + 1) * JS, :]).then_inc(bn_mid, 1)

                if not first:
                    if not (isinstance(i.k, int) and i.number() < 2):
                        dve.wait_ge(stored[i.buffer()], 16 * Q * (SLOTS // 2) * i.uses())
                    for s in range(SLOTS):
                        dve.wait_ge(c1_done, SLOTS * i.number() + s + 1)
                        nc.vector.scalar_tensor_tensor(
                            mid[:, i.buffer(), s * JS:(s + 1) * JS, :],
                            psum[:, s % BANKS, :].rearrange("p (j w) -> p j w", j=JS), unscale[:, 0:1],
                            x_even[:, i.buffer(), s * JS:(s + 1) * JS, :], ALU.mult, ALU.add).then_inc(c1_read, 1)
                        if s:
                            stats_mid(s - 1)
                    stats_mid(SLOTS - 1)
                if not last:
                    n = i + 1
                    dve.wait_ge(even_in[n.buffer()], 16 * Q * (n.uses() + 1))
                    for s in range(SLOTS):
                        nc.vector.bn_stats(bn[:, 0, s, :], x_even[:, n.buffer(), s * JS:(s + 1) * JS, :]).then_inc(bn_x, 1)
                    dve.wait_ge(bn_x, SLOTS * (n.number() + 1))
                    nc.vector.memset(carrier[:, 0:1], 0.0)
                    nc.vector.bn_aggr(mv[:, 0, :], bn[:, 0, :, :].rearrange("p s k -> p (s k)")).then_inc(stat_ready, 1)
                if not first:
                    dve.wait_ge(bn_mid, SLOTS * (i.number() + 1))
                    nc.vector.memset(carrier[:, 1:2], 0.0)
                    nc.vector.bn_aggr(mv[:, 1, :], bn[:, 1, :, :].rearrange("p s k -> p (s k)")).then_inc(stat_ready, 1)
                dve.wait_ge(stat_ready, 1 if first else 2 * N if last else 2 * i.number() + 3)
                c0, c1 = (0, 1) if first else (1, 2) if last else (0, 2)
                stage = i.number() + 1
                done = [0]

                def step(ins):
                    done[0] += 1
                    ins.then_inc(gstep, 1)
                    dve.wait_ge(gstep, STEPS_G * stage + done[0])

                dve.wait_ge(mean_mixed, stage + 1)
                step(nc.vector.tensor_copy(gmean[:, c0:c1], psum[:, B_MEAN, c0:c1]))
                step(nc.vector.tensor_tensor(spread[:, c0:c1], mv[:, c0:c1, 0], gmean[:, c0:c1], ALU.subtract))
                step(nc.vector.tensor_tensor(spread[:, c0:c1], spread[:, c0:c1], spread[:, c0:c1], ALU.mult))
                nc.vector.tensor_tensor(spread[:, c0:c1], spread[:, c0:c1], mv[:, c0:c1, 1], ALU.add).then_inc(spread_ready, 1)
                dve.wait_ge(var_mixed, stage + 1)
                nc.vector.tensor_scalar(gvar[:, c0:c1], psum[:, B_VAR, c0:c1], EPS, None, ALU.add).then_inc(var_ready, 1)
                dve.wait_ge(root_ready, stage + 1)
                step(nc.vector.reciprocal(rinv[:, c0:c1], root[:, c0:c1]))
                step(nc.vector.tensor_tensor(newton[:, c0:c1], gvar[:, c0:c1], rinv[:, c0:c1], ALU.mult))
                step(nc.vector.tensor_tensor(newton[:, c0:c1], newton[:, c0:c1], rinv[:, c0:c1], ALU.mult))
                step(nc.vector.tensor_scalar(newton[:, c0:c1], newton[:, c0:c1], -0.5, 1.5, ALU.mult, ALU.add))
                step(nc.vector.scalar_tensor_tensor(gscale[:, c0:c1], rinv[:, c0:c1], PIX * LOW, newton[:, c0:c1],
                                                    ALU.mult, ALU.mult))
                if not last:
                    dve.wait_ge(odd_in, 16 * Q * (stage + 1))
                    nc.vector.tensor_scalar(x_odd[0:C, 0, :], zrow[:, :], gmean[0:C, 0:1], None, ALU.add).then_inc(pad_set, 1)
                    dve.wait_ge(pad_set, stage + 1)
                steps = plan(first, last)
                flat = [(s, *t) for s in range(SLOTS) for t in steps.get(s, [])]
                for n in range(len(flat) + 1):
                    if n < len(flat):
                        normalize(*flat[n][1:], i)
                    if n:
                        low(*flat[n - 1][1:], i)

            turns(dve, turn)

        @block.tensor
        def _(pe):
            def over_partitions(col, src, n):
                nc.tensor.matmul(psum[:, B_SETUP, col:col + n], ones[:, :], src, start=True, stop=True).then_inc(w_summed, 1)

            pe.wait_ge(ones_set, 1)
            pe.wait_ge(wchain, 6)
            over_partitions(0, small[:, 1:2], 1)
            pe.wait_ge(wchain, 8 + T3 + 2)
            over_partitions(8, bound[:, 0:2], 2)
            pe.wait_ge(w_loaded, 16 * 14)

            def conv3(i, s):
                n = i
                pe.wait_ge(ready1, ITEMS1 * n + s // 2 + 1 + s % 2)
                products = [(p, dx) for p in range(3) for dx in range(K3)]
                for m, (p, dx) in enumerate(products):
                    for t in range(2):
                        src = ((a_hi, b_hi), (a_lo, b_lo), (a_hi, b_hi))[p][t]
                        last = nc.tensor.matmul(
                            psum[t * 2 * C:(t + 1) * 2 * C, s % BANKS, :].rearrange("p (j w) -> p j w", j=JS),
                            s3[:, p, dx, :], src[:, s * JS:(s + 1) * JS, 1 + dx:1 + dx + W],
                            start=(m == 0), stop=(m == len(products) - 1))
                last.then_inc(c1_done, 1)

            def conv5(i, s):
                pe.wait_ge(ready2, ITEMS2 * i + min(s + 2, SLOTS))
                products = [("pair", d, dx) for d in range(3) for dx in range(K5)]
                products += [("low", off, dx) for off in range(2) for dx in range(K5)]
                for m, (kind, d, dx) in enumerate(products):
                    for t in range(2):
                        if kind == "pair":
                            b, h = divmod(t + d, 2)
                            wt, src = s5_pair[:, d, dx, :], pairs[:, s * JS + b:(s + 1) * JS + b, h, dx:dx + W]
                        else:
                            b = t + d
                            wt, src = s5_low[:, t, d, dx, :], m_hi[:, s * JS + b:(s + 1) * JS + b, dx:dx + W]
                        last = nc.tensor.matmul(
                            psum[t * 2 * C:(t + 1) * 2 * C, s % BANKS, :].rearrange("p (j w) -> p j w", j=JS),
                            wt, src, start=(m == 0), stop=(m == len(products) - 1))
                last.then_inc(c2_done, 1)

            def mix_mean(i, c0, c1):
                pe.wait_ge(stat_ready, 2 * N if c0 else 1 if c1 == 1 else 2 * i + 3)
                nc.tensor.matmul(psum[:, B_MEAN, c0:c1], mix[:, :], mv[:, c0:c1, 0], start=True, stop=True).then_inc(mean_mixed, 1)

            def mix_var(i, c0, c1):
                pe.wait_ge(spread_ready, i + 2)
                nc.tensor.matmul(psum[:, B_VAR, c0:c1], mix[:, :], spread[:, c0:c1], start=True, stop=True).then_inc(var_mixed, 1)

            def turn(i, first=False, inner=False, last=False, end=False):
                c0, c1 = (0, 1) if first else (1, 2) if last else (0, 2)
                if not (first or end):
                    for s in range(SLOTS):
                        if s >= BANKS:
                            pe.wait_ge(c1_read, SLOTS * i + s + 1 - BANKS)
                        elif inner and not isinstance(i, int) or last or (isinstance(i, int) and i >= 2):
                            pe.wait_ge(c2_read, SLOTS * (i - 2) + s + 1 + BANKS)
                        conv3(i, s)
                if inner or last or end:
                    for s in range(SLOTS):
                        if s >= BANKS:
                            pe.wait_ge(c2_read, SLOTS * (i - 1) + s + 1 - BANKS)
                        elif end:
                            pe.wait_ge(c2_read, SLOTS * (i - 2) + s + 1 + BANKS)
                        else:
                            pe.wait_ge(c1_read, SLOTS * i + s + 1 + BANKS)
                        conv5(i - 1, s)
                        if s == 0 and not end:
                            mix_mean(i, c0, c1)
                        if s == 1 and not end:
                            mix_var(i, c0, c1)
                else:
                    mix_mean(i, c0, c1)
                    mix_var(i, c0, c1)

            turn(-1, first=True)
            pe.wait_ge(s3_set, 1)
            turn(0)
            pe.wait_ge(placed, 2 * 10 + 2 * 2 * K5)
            turn(1, inner=True)
            with pe.Fori(2, N - 1) as i:
                turn(i, inner=True)
            turn(N - 1, last=True)
            turn(N, end=True)


_INS = ["x", "L0_conv_weight", "L0_conv_threshold", "L1_conv_kernel", "L1_conv_bias"]


def kernel(**inputs):
    import numpy as np
    import concourse.bacc as bacc
    from concourse.bass_utils import run_bass_kernel_spmd as run

    nc = bacc.Bacc("TRN2", target_bir_lowering=False, num_devices=1)
    arrays, args = {}, []
    for name in _INS:
        a = np.ascontiguousarray(inputs[name])
        arrays[name + "_dram"] = a
        args.append(nc.dram_tensor(name + "_dram", a.shape, mybir.dt.from_np(a.dtype), kind="ExternalInput").ap())
    group = (np.arange(P) % C) // GROUP
    mix = (group[:, None] == group[None, :]).astype(np.float32) / (Q * GROUP)
    arrays["mix_dram"] = mix
    args.append(nc.dram_tensor("mix_dram", mix.shape, F32, kind="ExternalInput").ap())
    shape = arrays["x_dram"].shape
    args.append(nc.dram_tensor("out_dram", shape, F32, kind="ExternalOutput").ap())
    two_blocks(nc, *args)
    return run(nc, [arrays], core_ids=[0]).results[0]["out_dram"]
```

```python
from contextlib import ExitStack

import concourse.bass as bass
import concourse.mybir as mybir

F32 = mybir.dt.float32
F16 = mybir.dt.float16
U32 = mybir.dt.uint32
ALU = mybir.AluOpType
ACT = mybir.ActivationFunctionType
AX = mybir.AxisListType

C = 32
Q = 4
P = Q * C
K3, K5 = 3, 5
GROUP = 2
EPS = 1e-5
SLOTS = 8
BANKS = 4
B_MEAN, B_VAR, B_SETUP = 4, 5, 6
PIX = 2.0 ** 7
LOW = 2.0 ** 11
WTOP = 2.0 ** 14


class Image:

    def __init__(self, k, c):
        self.k, self.c = k, c

    def __add__(self, d):
        return Image(self.k, self.c + d)

    def number(self):
        return self.c if isinstance(self.k, int) and self.k == 0 else 2 * self.k + self.c

    def buffer(self):
        return self.c % 2

    def uses(self):
        return self.k + self.c // 2


def stationary5():
    found = []
    for o in range(2):
        for d in range(-1, 2):
            for r in range(2):
                dy = 2 * d + r - o + K5 // 2
                if 0 <= dy < K5:
                    found += [("pair", half + r, d + 1, o, dy, half // 2) for half in (0, 2)]
                    if d:
                        found += [("side", 2 * side + r, t, o, dy, side) for t in range(2) if d == 2 * t - 1
                                  for side in range(2)]
        for t in range(2):
            for q in range(Q):
                dy = q - 2 * t - o + K5 // 2
                if 0 <= dy < K5:
                    found.append(("low", q, t, o, dy, 0))
    return found


def two_blocks(nc, x, w3_dram, thr_dram, w5_dram, bias_dram, mix_dram, out):
    N, _, H, W = x.shape
    NJ = H // Q
    JS = NJ // SLOTS
    PITCH = W + 4
    T3, T5 = K3 * K3, K5 * K5
    DX2 = (K5 + 1) // 2

    with ExitStack() as ctx:
        def sbuf(name, shape, dt=F32):
            return ctx.enter_context(nc.sbuf_tensor(name, shape, dt))

        def sem(name):
            return ctx.enter_context(nc.semaphore(name))

        x_odd = sbuf("x_odd", [P, NJ + 1, W])
        x_even = sbuf("x_even", [P, 2, NJ, W])
        mid = sbuf("mid", [P, 2, NJ, W])
        conv_out = sbuf("conv_out", [P, BANKS, JS, W])
        a_hi = sbuf("a_hi", [P, NJ + 1, PITCH], F16)
        a_lo = sbuf("a_lo", [P, NJ + 1, PITCH], F16)
        b_hi = sbuf("b_hi", [P, NJ, PITCH], F16)
        b_lo = sbuf("b_lo", [P, NJ, PITCH], F16)
        m_hi = sbuf("m_hi", [P, NJ + 2, PITCH], F16)
        pairs = sbuf("pairs", [P, NJ + 1, 2, PITCH], F16)
        beside = sbuf("beside", [P, NJ + 1, 2, PITCH], F16)
        norm = sbuf("norm", [P, 2, NJ // 4, W])
        m_lo = sbuf("m_lo", [P, 2, NJ // 4, W], F16)
        mix = sbuf("mix", [P, P])
        bn = sbuf("bn", [P, 2, SLOTS, 6])
        mv = sbuf("mv", [P, 2, 2])
        gmean = sbuf("gmean", [P, 2, 2])
        spread = sbuf("spread", [P, 2])
        gvar = sbuf("gvar", [P, 2])
        root = sbuf("root", [P, 2])
        rinv = sbuf("rinv", [P, 2])
        newton = sbuf("newton", [P, 2])
        gscale = sbuf("gscale", [P, 2, 2])
        zrow = sbuf("zrow", [C, W])
        carrier = sbuf("carrier", [P, 2])
        w3 = sbuf("w3", [P, C, T3])
        w5 = sbuf("w5", [P, C, T5])
        w3n = sbuf("w3n", [P, C, T3])
        parts3 = [sbuf(f"w3_{n}", [P, C, T3], F16) for n in ("hi", "his", "lo")]
        parts5 = [sbuf(f"w5_{n}", [P, C, T5], F16) for n in ("hi", "his", "lo")]
        thr = sbuf("thr", [P, 1])
        bias = sbuf("bias", [P, 1])
        ones = sbuf("ones", [P, P])
        score = sbuf("score", [P, T3])
        mask = sbuf("mask", [P, T3])
        mask0 = sbuf("mask0", [P, T3])
        small = sbuf("small", [P, 8])
        bound = sbuf("bound", [P, 2])
        power = sbuf("power", [P, 2])
        wfac = sbuf("wfac", [P, 2])
        unscale = sbuf("unscale", [P, 2])
        s3 = sbuf("s3", [P, 3, K3, 2 * C], F16)
        s5_pair = sbuf("s5_pair", [P, 3, K5, 2 * C], F16)
        s5_low = sbuf("s5_low", [P, 2, K5, 2 * C], F16)
        s5_side = sbuf("s5_side", [P, 2, DX2, 2 * C], F16)
        psum = ctx.enter_context(nc.psum_tensor("psum", [P, 8, 512], F32))

        w3_loaded = sem("w3_loaded")
        w_loaded = sem("w_loaded")
        wstep = sem("wstep")
        wchain = sem("wchain")
        ones_set = sem("ones_set")
        zeroed = sem("zeroed")
        w_summed = sem("w_summed")
        w3_split = sem("w3_split")
        w5_split = sem("w5_split")
        s3_set = sem("s3_set")
        placed = sem("placed")
        odd_in = sem("odd_in")
        even_in = [sem("even_in0"), sem("even_in1")]
        stored = [[sem(f"stored{b}_{h}") for h in range(SLOTS // 2)] for b in range(2)]
        c1_done = sem("c1_done")
        c1_read = sem("c1_read")
        c2_done = sem("c2_done")
        c2_read = sem("c2_read")
        out_added = sem("out_added")
        bn_x = sem("bn_x")
        bn_mid = sem("bn_mid")
        stat_ready = sem("stat_ready")
        mean_mixed = sem("mean_mixed")
        spread_ready = sem("spread_ready")
        var_mixed = sem("var_mixed")
        var_ready = sem("var_ready")
        root_ready = sem("root_ready")
        gstep = sem("gstep")
        pad_set = sem("pad_set")
        norm1 = sem("norm1")
        hi1 = sem("hi1")
        b_set = sem("b_set")
        lo1 = sem("lo1")
        ready1 = sem("ready1")
        norm2 = sem("norm2")
        hi2 = sem("hi2")
        lo2 = sem("lo2")
        ready2 = sem("ready2")
        beside2 = sem("beside2")

        RUN = NJ // 4
        STEPS1 = 5
        STEPS2 = 4
        PLAN = {2: [(1, 0), (2, 0)], 3: [(1, 1)], 4: [(1, 2), (2, 1)], 5: [(1, 3), (1, 4)], 6: [(2, 2)]}

        def is_image(i, number):
            return isinstance(i.k, int) and i.number() == number

        def plan(i, first, last):
            if is_image(i, 0):
                return {2: [(1, j) for j in range(STEPS1)] + [(2, 0)]}
            return {s: [t for t in ts if not (t[0] == 2 and first) and not (t[0] == 1 and last)]
                    for s, ts in PLAN.items()}

        def left_over(i):
            return [1, 2, 3] if is_image(i, 1) else [3]

        STEPS_G = 8

        def turns(eng, turn):
            turn(Image(0, -1), first=True)
            turn(Image(0, 0))
            turn(Image(0, 1), inner=True)
            turn(Image(0, 2), inner=True)
            with eng.Fori(0, (N - 6) // 2) as k:
                turn(Image(k, 3), inner=True)
                turn(Image(k, 4), inner=True)
            turn(Image(0, N - 3), inner=True)
            turn(Image(0, N - 2), inner=True)
            turn(Image(0, N - 1), last=True)
            turn(Image(0, N), end=True)

        def rows(image, r):
            return image.rearrange("c (j q) w -> q c j w", q=Q)[r]

        block = ctx.enter_context(nc.Block())

        @block.sync
        def _(sp):
            def load_even(im):
                for q in range(Q):
                    nc.sync.dma_start(x_even[q * C:(q + 1) * C, im.buffer(), :, :],
                                      rows(x[im.number()], q)).then_inc(even_in[im.buffer()], 16)

            def load_odd(im):
                for q in range(Q):
                    first = 1 if q == 0 else 0
                    nc.sync.dma_start(x_odd[q * C:(q + 1) * C, first:first + NJ, :],
                                      rows(x[im.number()], (q + 3) % Q)).then_inc(odd_in, 16)

            for q in range(Q):
                part = slice(q * C, (q + 1) * C)
                sp.dma_start(w3[part, :, :], w3_dram.rearrange("o i a b -> i o (a b)")).then_inc(w3_loaded, 16)
            sp.dma_start(thr[:, :], thr_dram.rearrange("(a o) -> a o", a=1).to_broadcast([P, 1])).then_inc(w3_loaded, 16)
            load_even(Image(0, 0))
            for q in range(Q):
                part = slice(q * C, (q + 1) * C)
                sp.dma_start(w5[part, :, :], w5_dram.rearrange("o i a b -> i o (a b)")).then_inc(w_loaded, 16)
                sp.dma_start(bias[part, :], bias_dram.rearrange("(o a) -> o a", a=1)).then_inc(w_loaded, 16)
            sp.dma_start(mix[:, :], mix_dram).then_inc(w_loaded, 16)

            def turn(i, first=False, inner=False, last=False, end=False):
                if first:
                    load_odd(i + 1)
                    load_even(i + 2)
                    return
                if not (last or end):
                    sp.wait_ge(lo1, STEPS1 * (i.number() + 1))
                    sp.wait_ge(b_set, STEPS1 * (i.number() + 1))
                    load_odd(i + 1)
                    sp.wait_ge(c1_read, SLOTS * (i.number() + 1))
                    if not isinstance(i.k, int) or i.number() < N - 2:
                        load_even(i + 2)
                if inner or last or end:
                    o = i + -1
                    for s in range(0, SLOTS, 2):
                        sp.wait_ge(out_added, SLOTS * o.number() + s + 2)
                        for q in range(Q):
                            nc.sync.dma_start(
                                rows(out[o.number()], q)[:, s * JS:(s + 2) * JS, :],
                                mid[q * C:(q + 1) * C, o.buffer(), s * JS:(s + 2) * JS, :],
                            ).then_inc(stored[o.buffer()][s // 2], 16)

            turns(sp, turn)
            for of_buffer in stored:
                for quarter in of_buffer:
                    sp.wait_ge(quarter, 16 * Q * (N // 2))

        @block.gpsimd
        def _(pool):
            nc.gpsimd.memset(zrow[:, :], 0.0)
            for t in (a_hi, a_lo, b_hi, b_lo, m_hi):
                nc.gpsimd.memset(t[:, :, 0:2], 0.0)
                nc.gpsimd.memset(t[:, :, PITCH - 2:PITCH], 0.0)
            for t in (pairs, beside):
                nc.gpsimd.memset(t[:, :, :, 0:2], 0.0)
                nc.gpsimd.memset(t[:, :, :, PITCH - 3:PITCH], 0.0)
                nc.gpsimd.memset(t[:, 0, 0, 2:PITCH - 3], 0.0)
                nc.gpsimd.memset(t[:, NJ, 1, 2:PITCH - 3], 0.0)
            nc.gpsimd.memset(m_hi[:, 0, 2:2 + W], 0.0)
            nc.gpsimd.memset(m_hi[:, NJ + 1, 2:2 + W], 0.0)
            nc.gpsimd.memset(s5_pair[:, :, :, :], 0.0)
            nc.gpsimd.memset(s5_side[:, :, :, :], 0.0)
            nc.gpsimd.memset(s5_low[:, :, :, :], 0.0).then_inc(zeroed, 1)

            pool.wait_ge(w5_split, 3)
            pool.wait_ge(zeroed, 1)
            hi, his, lo = parts5
            copies = [0]

            def place(dst, src):
                nc.gpsimd.tensor_copy(dst, src).then_inc(placed, 1)
                copies[0] += 1
                pool.wait_ge(placed, copies[0])

            def taps(t, part, dy):
                return t[part, :, dy * K5:(dy + 1) * K5].rearrange("p o t -> p t o")

            for kind, q, at, o, dy, side in stationary5():
                part, col = slice(q * C, (q + 1) * C), slice(o * C, (o + 1) * C)
                if kind == "pair":
                    place(s5_pair[part, at, :, col], taps((hi, his)[side], part, dy))
                elif kind == "low":
                    place(s5_low[part, at, :, col], taps(lo, part, dy))
                else:
                    src = lo[part, :, dy * K5 + side:(dy + 1) * K5:2].rearrange("p o t -> p t o")
                    place(s5_side[part, at, 0:DX2 - side, col], src)

            def turn(o):
                for s in range(SLOTS):
                    pool.wait_ge(c2_read, SLOTS * o.number() + s + 1)
                    m = mid[:, o.buffer(), s * JS:(s + 1) * JS, :]
                    nc.gpsimd.tensor_tensor(m, m, conv_out[:, s % BANKS, :, :], ALU.add).then_inc(out_added, 1)

            with pool.Fori(0, N // 2) as k:
                turn(Image(k, 0))
                turn(Image(k, 1))

        @block.scalar
        def _(act):
            def high(which, j, i):
                if which == 1:
                    n = i + 1
                    act.wait_ge(norm1, STEPS1 * n.number() + j + 1)
                    if j < 4:
                        src = x_odd[:, j * RUN:(j + 1) * RUN, :]
                        dst = a_hi[:, j * RUN:(j + 1) * RUN, 2:2 + W]
                    else:
                        src = x_odd[0:C, NJ, :]
                        dst = a_hi[0:C, NJ, 2:2 + W]
                    nc.scalar.activation(dst, src, ACT.Copy, scale=1.0 / LOW).then_inc(hi1, 1)
                    b0, b1 = (j * RUN, (j + 1) * RUN) if j < 4 else (NJ, NJ + 1)
                    if j < 4:
                        nc.scalar.activation(b_hi[0:2 * C, b0:b1, 2:2 + W], x_odd[2 * C:P, b0:b1, :],
                                             ACT.Copy, scale=1.0 / LOW)
                    b0 = max(b0, 1)
                    half = 2 * C if j < 4 else C
                    nc.scalar.activation(b_hi[2 * C:2 * C + half, b0 - 1:b1 - 1, 2:2 + W], x_odd[0:half, b0:b1, :],
                                         ACT.Copy, scale=1.0 / LOW).then_inc(b_set, 1)
                else:
                    act.wait_ge(norm2, STEPS2 * i.number() + j + 1)
                    nc.scalar.activation(m_hi[:, 1 + j * RUN:1 + (j + 1) * RUN, 2:2 + W], norm[:, j % 2, :, :],
                                         ACT.Copy, scale=1.0 / LOW).then_inc(hi2, 1)
                    for t in range(2):
                        last = nc.scalar.activation(beside[2 * C:P, j * RUN + t:(j + 1) * RUN + t, 1 - t, 1:1 + W],
                                                    norm[2 * C * t:2 * C * (t + 1), j % 2, :, :],
                                                    ACT.Copy, scale=1.0 / LOW)
                    last.then_inc(beside2, 1)

            def turn(i, first=False, inner=False, last=False, end=False):
                o = i + -1
                steps = plan(i, first, last)
                if inner or last or end:
                    for j in left_over(i):
                        high(2, j, o)
                for s in range(SLOTS):
                    if inner or last or end:
                        if s == 0 and isinstance(o.k, int) and o.number() == 0:
                            act.wait_ge(wstep, 1)
                        act.wait_ge(c2_done, SLOTS * o.number() + s + 1)
                        if s >= BANKS or not (isinstance(o.k, int) and o.number() == 0):
                            act.wait_ge(out_added, SLOTS * o.number() + s + 1 - BANKS)
                        nc.scalar.activation(conv_out[:, s % BANKS, :, :],
                                             psum[:, s % BANKS, :].rearrange("p (j w) -> p j w", j=JS),
                                             ACT.Identity, bias=bias[:, 0:1], scale=unscale[:, 1:2]).then_inc(c2_read, 1)
                    if end:
                        continue
                    if s == 2:
                        act.wait_ge(var_ready, i.number() + 2)
                        c0, c1 = (0, 1) if first else (1, 2) if last else (0, 2)
                        nc.scalar.activation(root[:, c0:c1], gvar[:, c0:c1], ACT.Sqrt).then_inc(root_ready, 1)
                    for which, j in steps.get(s, []):
                        high(which, j, i)

            turns(act, turn)

        @block.vector
        def _(dve):
            nc.vector.memset(ones[:, :], 1.0).then_inc(ones_set, 1)
            nc.vector.memset(s3[:, :, :, :], 0.0)
            for t in (b_hi, b_lo):
                nc.vector.memset(t[P - C:P, NJ - 1, 2:2 + W], 0.0)
            steps_w = [0]

            def own_step(ins):
                steps_w[0] += 1
                ins.then_inc(wchain, 1)
                dve.wait_ge(wchain, steps_w[0])

            def input_stats(n):
                dve.wait_ge(even_in[n.buffer()], 16 * Q * (n.uses() + 1))
                for s in range(SLOTS):
                    nc.vector.bn_stats(bn[:, 0, s, :], x_even[:, n.buffer(), s * JS:(s + 1) * JS, :]).then_inc(bn_x, 1)

            def split_weights(w, n, parts, split):
                hi, his, lo = parts
                own_step(nc.vector.tensor_scalar(w[:, :, :], w[:, :, :], wfac[:, n:n + 1], None, ALU.mult))
                own_step(nc.vector.tensor_copy(hi[:, :, :], w[:, :, :]))
                nc.vector.tensor_scalar(his[:, :, :], hi[:, :, :], 1.0 / LOW, None, ALU.mult).then_inc(split, 1)
                nc.vector.tensor_tensor(lo[:, :, :], w[:, :, :], hi[:, :, :], ALU.subtract).then_inc(split, 2)

            def largest(w, n):
                own_step(nc.vector.tensor_reduce(bound[:, n:n + 1], w[:, :, :].rearrange("p o t -> p (o t)"), AX.X,
                                                 ALU.max, apply_absolute_value=True))

            def power_of_two(n, sums):
                at = slice(n, n + 1)
                dve.wait_ge(w_summed, sums)
                own_step(nc.vector.tensor_scalar(power[:, at], psum[:, B_SETUP, 8 + n:9 + n], 2.0 ** -100, None, ALU.max))
                own_step(nc.vector.tensor_scalar(power[:, at].bitcast(U32), power[:, at].bitcast(U32), 0x7F800000, None,
                                                 ALU.bitwise_and))
                own_step(nc.vector.reciprocal(wfac[:, at], power[:, at]))
                own_step(nc.vector.tensor_scalar(wfac[:, at], wfac[:, at], WTOP, None, ALU.mult))
                own_step(nc.vector.tensor_scalar(unscale[:, at], power[:, at], 1.0 / (WTOP * PIX), None, ALU.mult))

            def setup3():
                dve.wait_ge(w3_loaded, 16 * (Q + 1))
                own_step(nc.vector.tensor_reduce(score[:, :], w3[:, :, :].rearrange("p o t -> p t o"), AX.X, ALU.add,
                                                 apply_absolute_value=True))
                own_step(nc.vector.tensor_scalar(small[:, 0:1], thr[:, :], 0.0, None, ALU.max))
                own_step(nc.vector.tensor_scalar(mask[:, :], score[:, :], 1.0 / C, small[:, 0:1], ALU.mult, ALU.subtract))
                own_step(nc.vector.tensor_scalar(mask[:, :], mask[:, :], 0.0, None, ALU.is_gt))
                own_step(nc.vector.tensor_scalar(mask0[:, :], score[:, :], 1.0 / C, 0.0, ALU.mult, ALU.is_gt))
                own_step(nc.vector.tensor_reduce(small[:, 1:2], mask[:, :], AX.X, ALU.add))
                dve.wait_ge(w_summed, 1)
                own_step(nc.vector.tensor_scalar(small[:, 2:3], psum[:, B_SETUP, 0:1], 1.0 / (Q * C * T3), 0.01,
                                                 ALU.mult, ALU.is_le))
                own_step(nc.vector.scalar_tensor_tensor(mask[:, :], mask0[:, :], small[:, 2:3], mask[:, :], ALU.mult, ALU.max))
                for t in range(T3):
                    ins = nc.vector.tensor_scalar(w3n[:, :, t], w3[:, :, t], mask[:, t:t + 1], None, ALU.mult)
                own_step(ins)
                largest(w3n, 0)
                power_of_two(0, 2)
                split_weights(w3n, 0, parts3, w3_split)
                dve.wait_ge(w3_split, 3)
                for n, t in enumerate(parts3):
                    for q in range(Q):
                        for o in range(2):
                            if 0 <= q - o < K3:
                                part = slice(q * C, (q + 1) * C)
                                last = nc.vector.tensor_copy(
                                    s3[part, n, :, o * C:(o + 1) * C],
                                    t[part, :, (q - o) * K3:(q - o + 1) * K3].rearrange("p o t -> p t o"))
                last.then_inc(s3_set, 1)

            def setup5():
                power_of_two(1, 3)
                split_weights(w5, 1, parts5, w5_split)
                nc.vector.memset(small[:, 3:4], 0.0).then_inc(wstep, 1)

            def normalize(which, j, i):
                if which == 1:
                    if j < 4:
                        v = x_odd[:, j * RUN:(j + 1) * RUN, :]
                        m, s = gmean[:, i.buffer(), 0:1], gscale[:, i.buffer(), 0:1]
                    else:
                        v = x_odd[0:C, NJ, :]
                        m, s = gmean[0:C, i.buffer(), 0:1], gscale[0:C, i.buffer(), 0:1]
                    nc.vector.tensor_scalar(v, v, m, s, ALU.subtract, ALU.mult).then_inc(norm1, 1)
                else:
                    if j >= 2 or not (isinstance(i.k, int) and i.number() == 0):
                        dve.wait_ge(beside2, STEPS2 * i.number() + j - 1)
                    nc.vector.tensor_scalar(norm[:, j % 2, :, :], mid[:, i.buffer(), j * RUN:(j + 1) * RUN, :],
                                            gmean[:, i.buffer(), 1:2], gscale[:, i.buffer(), 1:2], ALU.subtract, ALU.mult).then_inc(norm2, 1)

            def low(which, j, i):
                if which == 1:
                    n = i + 1
                    count = STEPS1 * n.number() + j + 1
                    dve.wait_ge(hi1, count)
                    if j < 4:
                        part, b0, b1 = slice(0, P), j * RUN, (j + 1) * RUN
                    else:
                        part, b0, b1 = slice(0, C), NJ, NJ + 1
                    nc.vector.scalar_tensor_tensor(a_lo[part, b0:b1, 2:2 + W], a_hi[part, b0:b1, 2:2 + W], -LOW,
                                                   x_odd[part, b0:b1, :], ALU.mult, ALU.add).then_inc(lo1, 1)
                    dve.wait_ge(lo1, count)
                    if j < 4:
                        nc.vector.tensor_copy(b_lo[0:2 * C, b0:b1, 2:2 + W], a_lo[2 * C:P, b0:b1, 2:2 + W])
                    first = max(b0, 1)
                    half = 2 * C if j < 4 else C
                    nc.vector.tensor_copy(b_lo[2 * C:2 * C + half, first - 1:b1 - 1, 2:2 + W],
                                          a_lo[0:half, first:b1, 2:2 + W]).then_inc(ready1, 1)
                else:
                    count = STEPS2 * i.number() + j + 1
                    blocks = slice(1 + j * RUN, 1 + (j + 1) * RUN)
                    dve.wait_ge(hi2, count)
                    nc.vector.scalar_tensor_tensor(m_lo[:, j % 2, :, :], m_hi[:, blocks, 2:2 + W],
                                                   -LOW, norm[:, j % 2, :, :], ALU.mult, ALU.add).then_inc(lo2, 1)
                    for t in range(2):
                        at, src = slice(j * RUN + t, (j + 1) * RUN + t), slice(2 * C * t, 2 * C * (t + 1))
                        for dst in (pairs, beside):
                            nc.vector.tensor_copy(dst[0:2 * C, at, 1 - t, 2:2 + W], m_hi[src, blocks, 2:2 + W])
                    dve.wait_ge(lo2, count)
                    for t in range(2):
                        at, src = slice(j * RUN + t, (j + 1) * RUN + t), slice(2 * C * t, 2 * C * (t + 1))
                        last = nc.vector.tensor_copy(pairs[2 * C:P, at, 1 - t, 2:2 + W], m_lo[src, j % 2, :, :])
                    last.then_inc(ready2, 1)

            def left(i, steps):
                for n, j in enumerate(steps):
                    normalize(2, j, i + -1)
                    if n:
                        low(2, steps[n - 1], i + -1)
                low(2, steps[-1], i + -1)

            def turn(i, first=False, inner=False, last=False, end=False):
                if end:
                    left(i, left_over(i))
                    return
                if first:
                    setup3()
                    dve.wait_ge(w_loaded, 16 * (2 * Q + 1))
                    largest(w5, 1)
                    input_stats(i + 1)
                elif isinstance(i.k, int) and i.number() == 0:
                    setup5()
                def stats_mid(s):
                    dve.wait_ge(c1_read, SLOTS * i.number() + s + 1)
                    nc.vector.bn_stats(bn[:, 1, s, :], mid[:, i.buffer(), s * JS:(s + 1) * JS, :]).then_inc(bn_mid, 1)

                if not first:
                    for s in range(SLOTS):
                        if s % 2 == 0 and not (isinstance(i.k, int) and i.number() < 2):
                            dve.wait_ge(stored[i.buffer()][s // 2], 16 * Q * i.uses())
                        dve.wait_ge(c1_done, SLOTS * i.number() + s + 1)
                        nc.vector.scalar_tensor_tensor(
                            mid[:, i.buffer(), s * JS:(s + 1) * JS, :],
                            psum[:, s % BANKS, :].rearrange("p (j w) -> p j w", j=JS), unscale[:, 0:1],
                            x_even[:, i.buffer(), s * JS:(s + 1) * JS, :], ALU.mult, ALU.add).then_inc(c1_read, 1)
                        if s:
                            stats_mid(s - 1)
                    stats_mid(SLOTS - 1)
                if not last:
                    n = i + 1
                    dve.wait_ge(bn_x, SLOTS * (n.number() + 1))
                    nc.vector.memset(carrier[:, 0:1], 0.0)
                    nc.vector.bn_aggr(mv[:, 0, :], bn[:, 0, :, :].rearrange("p s k -> p (s k)")).then_inc(stat_ready, 1)
                if not first:
                    dve.wait_ge(bn_mid, SLOTS * (i.number() + 1))
                    nc.vector.memset(carrier[:, 1:2], 0.0)
                    nc.vector.bn_aggr(mv[:, 1, :], bn[:, 1, :, :].rearrange("p s k -> p (s k)")).then_inc(stat_ready, 1)
                if is_image(i, 1):
                    left(i, left_over(i))
                c0, c1 = (0, 1) if first else (1, 2) if last else (0, 2)
                stage = i.number() + 1
                done = [0]

                def step(ins):
                    done[0] += 1
                    ins.then_inc(gstep, 1)
                    dve.wait_ge(gstep, STEPS_G * stage + done[0])

                dve.wait_ge(stat_ready, 1 if first else 2 * N if last else 2 * i.number() + 3)
                dve.wait_ge(mean_mixed, stage + 1)
                step(nc.vector.tensor_copy(gmean[:, i.buffer(), c0:c1], psum[:, B_MEAN, c0:c1]))
                step(nc.vector.tensor_tensor(spread[:, c0:c1], mv[:, c0:c1, 0], gmean[:, i.buffer(), c0:c1], ALU.subtract))
                step(nc.vector.tensor_tensor(spread[:, c0:c1], spread[:, c0:c1], spread[:, c0:c1], ALU.mult))
                nc.vector.tensor_tensor(spread[:, c0:c1], spread[:, c0:c1], mv[:, c0:c1, 1], ALU.add).then_inc(spread_ready, 1)
                if (inner or last) and not is_image(i, 1):
                    left(i, left_over(i))
                dve.wait_ge(var_mixed, stage + 1)
                nc.vector.tensor_scalar(gvar[:, c0:c1], psum[:, B_VAR, c0:c1], EPS, None, ALU.add).then_inc(var_ready, 1)
                dve.wait_ge(root_ready, stage + 1)
                step(nc.vector.reciprocal(rinv[:, c0:c1], root[:, c0:c1]))
                step(nc.vector.tensor_tensor(newton[:, c0:c1], gvar[:, c0:c1], rinv[:, c0:c1], ALU.mult))
                step(nc.vector.tensor_tensor(newton[:, c0:c1], newton[:, c0:c1], rinv[:, c0:c1], ALU.mult))
                step(nc.vector.tensor_scalar(newton[:, c0:c1], newton[:, c0:c1], -0.5, 1.5, ALU.mult, ALU.add))
                step(nc.vector.scalar_tensor_tensor(gscale[:, i.buffer(), c0:c1], rinv[:, c0:c1], PIX * LOW, newton[:, c0:c1],
                                                    ALU.mult, ALU.mult))
                if first:
                    dve.wait_ge(zeroed, 1)
                if not last:
                    dve.wait_ge(odd_in, 16 * Q * (stage + 1))
                    nc.vector.tensor_scalar(x_odd[0:C, 0, :], zrow[:, :], gmean[0:C, i.buffer(), 0:1], None, ALU.add).then_inc(pad_set, 1)
                    dve.wait_ge(pad_set, stage + 1)
                steps = plan(i, first, last)
                flat = [(s, *t) for s in range(SLOTS) for t in steps.get(s, [])]
                ahead = not (isinstance(i.k, int) and i.number() > N - 3)
                for n in range(len(flat) + 1):
                    if n < len(flat):
                        normalize(*flat[n][1:], i)
                    if n:
                        low(*flat[n - 1][1:], i)
                    if ahead and n == (len(flat) if first else len(flat) - 2):
                        input_stats(i + 2)

            turns(dve, turn)

        @block.tensor
        def _(pe):
            def over_partitions(col, src, n):
                nc.tensor.matmul(psum[:, B_SETUP, col:col + n], ones[:, :], src, start=True, stop=True).then_inc(w_summed, 1)

            pe.wait_ge(ones_set, 1)
            pe.wait_ge(wchain, 6)
            over_partitions(0, small[:, 1:2], 1)
            pe.wait_ge(wchain, 10)
            over_partitions(8, bound[:, 0:1], 1)
            pe.wait_ge(w_loaded, 16 * (2 * Q + 1))

            def conv3(i, s):
                n = i
                pe.wait_ge(ready1, STEPS1 * n + s // 2 + 1 + s % 2)
                pe.wait_ge(b_set, STEPS1 * n + s // 2 + 1 + s % 2)
                products = [(p, dx) for p in range(3) for dx in range(K3)]
                for m, (p, dx) in enumerate(products):
                    for t in range(2):
                        src = ((a_hi, b_hi), (a_lo, b_lo), (a_hi, b_hi))[p][t]
                        last = nc.tensor.matmul(
                            psum[t * 2 * C:(t + 1) * 2 * C, s % BANKS, :].rearrange("p (j w) -> p j w", j=JS),
                            s3[:, p, dx, :], src[:, s * JS:(s + 1) * JS, 1 + dx:1 + dx + W],
                            start=(m == 0), stop=(m == len(products) - 1))
                last.then_inc(c1_done, 1)

            def conv5(i, s):
                runs = min((s + 1) * JS // RUN + 1, STEPS2)
                pe.wait_ge(ready2, STEPS2 * i + runs)
                pe.wait_ge(beside2, STEPS2 * i + runs)
                products = [("pair", d, dx) for d in range(3) for dx in range(K5)]
                products += [("low", 0, dx) for dx in range(K5)] + [("side", 0, dx) for dx in range(0, K5, 2)]
                for m, (kind, d, dx) in enumerate(products):
                    for t in range(2):
                        if kind == "pair":
                            b, h = divmod(t + d, 2)
                            wt, src = s5_pair[:, d, dx, :], pairs[:, s * JS + b:(s + 1) * JS + b, h, dx:dx + W]
                        elif kind == "low":
                            wt, src = s5_low[:, t, dx, :], m_hi[:, s * JS + 1:(s + 1) * JS + 1, dx:dx + W]
                        else:
                            wt = s5_side[:, t, dx // 2, :]
                            src = beside[:, s * JS + t:(s + 1) * JS + t, t, dx:dx + W]
                        last = nc.tensor.matmul(
                            psum[t * 2 * C:(t + 1) * 2 * C, s % BANKS, :].rearrange("p (j w) -> p j w", j=JS),
                            wt, src, start=(m == 0), stop=(m == len(products) - 1))
                last.then_inc(c2_done, 1)

            def mix_mean(i, c0, c1):
                pe.wait_ge(stat_ready, 2 * N if c0 else 1 if c1 == 1 else 2 * i + 3)
                nc.tensor.matmul(psum[:, B_MEAN, c0:c1], mix[:, :], mv[:, c0:c1, 0], start=True, stop=True).then_inc(mean_mixed, 1)

            def mix_var(i, c0, c1):
                pe.wait_ge(spread_ready, i + 2)
                nc.tensor.matmul(psum[:, B_VAR, c0:c1], mix[:, :], spread[:, c0:c1], start=True, stop=True).then_inc(var_mixed, 1)

            def turn(i, first=False, inner=False, last=False, end=False):
                c0, c1 = (0, 1) if first else (1, 2) if last else (0, 2)
                if not (first or end):
                    for s in range(SLOTS):
                        if s >= BANKS:
                            pe.wait_ge(c1_read, SLOTS * i + s + 1 - BANKS)
                        elif inner and not isinstance(i, int) or last or (isinstance(i, int) and i >= 2):
                            pe.wait_ge(c2_read, SLOTS * (i - 2) + s + 1 + BANKS)
                        conv3(i, s)
                if isinstance(i, int) and i == 1:
                    pe.wait_ge(placed, len(stationary5()))
                if inner or last or end:
                    for s in range(SLOTS):
                        if s >= BANKS:
                            pe.wait_ge(c2_read, SLOTS * (i - 1) + s + 1 - BANKS)
                        elif end:
                            pe.wait_ge(c2_read, SLOTS * (i - 2) + s + 1 + BANKS)
                        else:
                            pe.wait_ge(c1_read, SLOTS * i + s + 1 + BANKS)
                        conv5(i - 1, s)
                        if s == 0 and not end:
                            mix_mean(i, c0, c1)
                        if s == 1 and not end:
                            mix_var(i, c0, c1)
                else:
                    mix_mean(i, c0, c1)
                    mix_var(i, c0, c1)

            pe.wait_ge(wchain, 18)
            over_partitions(9, bound[:, 1:2], 1)
            turn(-1, first=True)
            pe.wait_ge(s3_set, 1)
            turn(0)
            turn(1, inner=True)
            with pe.Fori(2, N - 1) as i:
                turn(i, inner=True)
            turn(N - 1, last=True)
            turn(N, end=True)


_INS = ["x", "L0_conv_weight", "L0_conv_threshold", "L1_conv_kernel", "L1_conv_bias"]


def kernel(**inputs):
    import numpy as np
    import concourse.bacc as bacc
    from concourse.bass_utils import run_bass_kernel_spmd as run

    nc = bacc.Bacc("TRN2", target_bir_lowering=False, num_devices=1)
    arrays, args = {}, []
    for name in _INS:
        a = np.ascontiguousarray(inputs[name])
        arrays[name + "_dram"] = a
        args.append(nc.dram_tensor(name + "_dram", a.shape, mybir.dt.from_np(a.dtype), kind="ExternalInput").ap())
    group = (np.arange(P) % C) // GROUP
    mix = (group[:, None] == group[None, :]).astype(np.float32) / (Q * GROUP)
    arrays["mix_dram"] = mix
    args.append(nc.dram_tensor("mix_dram", mix.shape, F32, kind="ExternalInput").ap())
    shape = arrays["x_dram"].shape
    args.append(nc.dram_tensor("out_dram", shape, F32, kind="ExternalOutput").ap())
    two_blocks(nc, *args)
    return run(nc, [arrays], core_ids=[0]).results[0]["out_dram"]
```

```python
from contextlib import ExitStack

import concourse.bass as bass
import concourse.mybir as mybir

F32 = mybir.dt.float32
F16 = mybir.dt.float16
U32 = mybir.dt.uint32
ALU = mybir.AluOpType
ACT = mybir.ActivationFunctionType
AX = mybir.AxisListType

C = 32
Q = 4
P = Q * C
K3, K5 = 3, 5
GROUP = 2
EPS = 1e-5
SLOTS = 8
BANKS = 4
B_MEAN, B_VAR, B_SETUP, B_SPARE = 4, 5, 6, 7
PIX = 2.0 ** 7
LOW = 2.0 ** 11
WTOP = 2.0 ** 14


class Image:

    def __init__(self, k, c):
        self.k, self.c = k, c

    def __add__(self, d):
        return Image(self.k, self.c + d)

    def number(self):
        return self.c if isinstance(self.k, int) and self.k == 0 else 2 * self.k + self.c

    def buffer(self):
        return self.c % 2

    def uses(self):
        return self.k + self.c // 2


def stationary5():
    found = []
    for o in range(2):
        for d in range(-1, 2):
            for r in range(2):
                dy = 2 * d + r - o + K5 // 2
                if 0 <= dy < K5:
                    found += [("pair", half + r, d + 1, o, dy, half // 2) for half in (0, 2)]
                    if d:
                        found += [("side", 2 * side + r, t, o, dy, side) for t in range(2) if d == 2 * t - 1
                                  for side in range(2)]
        for t in range(2):
            for q in range(Q):
                dy = q - 2 * t - o + K5 // 2
                if 0 <= dy < K5:
                    found.append(("low", q, t, o, dy, 0))
    return found


def two_blocks(nc, x, w3_dram, thr_dram, w5_dram, bias_dram, mix_dram, out):
    N, _, H, W = x.shape
    NJ = H // Q
    JS = NJ // SLOTS
    PITCH = W + 4
    T3, T5 = K3 * K3, K5 * K5
    DX2 = (K5 + 1) // 2

    with ExitStack() as ctx:
        def sbuf(name, shape, dt=F32):
            return ctx.enter_context(nc.sbuf_tensor(name, shape, dt))

        def sem(name):
            return ctx.enter_context(nc.semaphore(name))

        x_odd = sbuf("x_odd", [P, NJ + 1, W])
        x_even = sbuf("x_even", [P, 2, NJ, W])
        mid = sbuf("mid", [P, 2, NJ, W])
        conv_out = sbuf("conv_out", [P, BANKS, JS, W])
        a_hi = sbuf("a_hi", [P, NJ + 1, PITCH], F16)
        a_lo = sbuf("a_lo", [P, NJ + 1, PITCH], F16)
        b_hi = sbuf("b_hi", [P, NJ, PITCH], F16)
        b_lo = sbuf("b_lo", [P, NJ, PITCH], F16)
        m_hi = sbuf("m_hi", [P, NJ + 2, PITCH], F16)
        pairs = sbuf("pairs", [P, NJ + 1, 2, PITCH], F16)
        beside = sbuf("beside", [P, NJ + 1, 2, PITCH], F16)
        norm = sbuf("norm", [P, 2, NJ // 4, W])
        m_lo = sbuf("m_lo", [P, 2, NJ // 4, W], F16)
        mix = sbuf("mix", [P, P])
        bn = sbuf("bn", [P, 2, SLOTS, 6])
        mv = sbuf("mv", [P, 2, 2])
        gmean = sbuf("gmean", [P, 2, 2])
        spread = sbuf("spread", [P, 2])
        gvar = sbuf("gvar", [P, 2])
        root = sbuf("root", [P, 2])
        rinv = sbuf("rinv", [P, 2])
        newton = sbuf("newton", [P, 2])
        gscale = sbuf("gscale", [P, 2, 2])
        zrow = sbuf("zrow", [C, W])
        carrier = sbuf("carrier", [P, 2])
        w3 = sbuf("w3", [P, C, T3])
        w5 = sbuf("w5", [P, C, T5])
        w3n = sbuf("w3n", [P, C, T3])
        parts3 = [sbuf(f"w3_{n}", [P, C, T3], F16) for n in ("hi", "his", "lo")]
        parts5 = [sbuf(f"w5_{n}", [P, C, T5], F16) for n in ("hi", "his", "lo")]
        thr = sbuf("thr", [P, 1])
        bias = sbuf("bias", [P, 1])
        ones = sbuf("ones", [P, P])
        score = sbuf("score", [P, T3])
        mask = sbuf("mask", [P, T3])
        mask0 = sbuf("mask0", [P, T3])
        small = sbuf("small", [P, 8])
        bound = sbuf("bound", [P, 2])
        power = sbuf("power", [P, 2])
        wfac = sbuf("wfac", [P, 2])
        unscale = sbuf("unscale", [P, 2])
        s3 = sbuf("s3", [P, 3, K3, 2 * C], F16)
        s5_pair = sbuf("s5_pair", [P, 3, K5, 2 * C], F16)
        s5_low = sbuf("s5_low", [P, 2, K5, 2 * C], F16)
        s5_side = sbuf("s5_side", [P, 2, DX2, 2 * C], F16)
        psum = ctx.enter_context(nc.psum_tensor("psum", [P, 8, 512], F32))

        w3_loaded = sem("w3_loaded")
        w_loaded = sem("w_loaded")
        kept_counted = sem("kept_counted")
        w_bound = sem("w_bound")
        w5_bounded = sem("w5_bounded")
        s3_zero = sem("s3_zero")
        wchain = sem("wchain")
        ones_set = sem("ones_set")
        zeroed = sem("zeroed")
        w_summed = sem("w_summed")
        w3_split = sem("w3_split")
        w5_split = sem("w5_split")
        s3_set = sem("s3_set")
        placed = sem("placed")
        odd_in = sem("odd_in")
        first_half_in = sem("first_half_in")
        even_in = [sem("even_in0"), sem("even_in1")]
        stored = [[sem(f"stored{b}_{h}") for h in range(SLOTS // 2)] for b in range(2)]
        c1_done = sem("c1_done")
        c1_read = sem("c1_read")
        c2_done = sem("c2_done")
        c2_read = sem("c2_read")
        out_added = sem("out_added")
        bn_x = sem("bn_x")
        bn_mid = sem("bn_mid")
        stat_ready = sem("stat_ready")
        mean_mixed = sem("mean_mixed")
        spread_ready = sem("spread_ready")
        var_mixed = sem("var_mixed")
        var_ready = sem("var_ready")
        root_ready = sem("root_ready")
        gstep = sem("gstep")
        pad_set = sem("pad_set")
        norm1 = sem("norm1")
        hi1 = sem("hi1")
        b_set = sem("b_set")
        lo1 = sem("lo1")
        ready1 = sem("ready1")
        norm2 = sem("norm2")
        hi2 = sem("hi2")
        lo2 = sem("lo2")
        ready2 = sem("ready2")
        beside2 = sem("beside2")

        RUN = NJ // 4
        STEPS1 = 5
        STEPS2 = 4
        PLAN = {2: [(1, 0), (2, 0)], 3: [(1, 1)], 4: [(1, 2), (2, 1)], 5: [(1, 3), (1, 4)], 6: [(2, 2)]}

        def is_image(i, number):
            return isinstance(i.k, int) and i.number() == number

        def plan(i, first, last):
            if is_image(i, 0):
                return {EARLY - 1: [(2, 0), (2, 1)] + [(1, j) for j in range(STEPS1)]}
            if is_image(i, 1):
                return {4: [(1, 0)], 5: [(1, 1), (1, 2)], 6: [(1, 3), (1, 4)], 7: [(2, 0), (2, 1)]}
            return {s: [t for t in ts if not (t[0] == 2 and first) and not (t[0] == 1 and last)]
                    for s, ts in PLAN.items()}

        def left_over(i):
            return [2, 3] if is_image(i, 1) or is_image(i, 2) else [3]

        EARLY = 3

        def mix_at(number):
            return EARLY if isinstance(number, int) and number == 1 else 0

        def root_at(i):
            return EARLY + 1 if is_image(i, 1) else 2

        STATS_BEHIND = {0: [(0, 1), (2, 3), (4, 5), (6,), (7,), (), (), ()], 2: [(s,) for s in range(SLOTS)]}
        STEPS_G = 8

        def turns(eng, turn):
            turn(Image(0, -1), first=True)
            turn(Image(0, 0))
            turn(Image(0, 1), inner=True)
            turn(Image(0, 2), inner=True)
            with eng.Fori(0, (N - 6) // 2) as k:
                turn(Image(k, 3), inner=True)
                turn(Image(k, 4), inner=True)
            turn(Image(0, N - 3), inner=True)
            turn(Image(0, N - 2), inner=True)
            turn(Image(0, N - 1), last=True)
            turn(Image(0, N), end=True)

        def rows(image, r):
            return image.rearrange("c (j q) w -> q c j w", q=Q)[r]

        block = ctx.enter_context(nc.Block())

        @block.sync
        def _(sp):
            def load_first_even():
                for h in range(2):
                    blocks = slice(h * NJ // 2, (h + 1) * NJ // 2)
                    for q in range(Q):
                        nc.sync.dma_start(x_even[q * C:(q + 1) * C, 0, blocks, :], rows(x[0], q)[:, blocks, :],
                                          ).then_inc(first_half_in if h == 0 else even_in[0], 16)

            def load_even(im):
                for q in range(Q):
                    nc.sync.dma_start(x_even[q * C:(q + 1) * C, im.buffer(), :, :],
                                      rows(x[im.number()], q)).then_inc(even_in[im.buffer()], 16)

            def load_odd(im):
                for q in range(Q):
                    first = 1 if q == 0 else 0
                    nc.sync.dma_start(x_odd[q * C:(q + 1) * C, first:first + NJ, :],
                                      rows(x[im.number()], (q + 3) % Q)).then_inc(odd_in, 16)

            for q in range(Q):
                part = slice(q * C, (q + 1) * C)
                sp.dma_start(w3[part, :, :], w3_dram.rearrange("o i a b -> i o (a b)")).then_inc(w3_loaded, 16)
            sp.dma_start(thr[:, :], thr_dram.rearrange("(a o) -> a o", a=1).to_broadcast([P, 1])).then_inc(w3_loaded, 16)
            for q in range(Q):
                part = slice(q * C, (q + 1) * C)
                sp.dma_start(w5[part, :, :], w5_dram.rearrange("o i a b -> i o (a b)")).then_inc(w_loaded, 16)
                sp.dma_start(bias[part, :], bias_dram.rearrange("(o a) -> o a", a=1)).then_inc(w_loaded, 16)
            sp.dma_start(mix[:, :], mix_dram).then_inc(w_loaded, 16)
            load_first_even()

            def turn(i, first=False, inner=False, last=False, end=False):
                if first:
                    load_odd(i + 1)
                    load_even(i + 2)
                    return
                if not (last or end):
                    sp.wait_ge(lo1, STEPS1 * (i.number() + 1))
                    sp.wait_ge(b_set, STEPS1 * (i.number() + 1))
                    load_odd(i + 1)
                    sp.wait_ge(c1_read, SLOTS * (i.number() + 1))
                    if not isinstance(i.k, int) or i.number() < N - 2:
                        load_even(i + 2)
                if inner or last or end:
                    o = i + -1
                    for s in range(0, SLOTS, 2):
                        sp.wait_ge(out_added, SLOTS * o.number() + s + 2)
                        for q in range(Q):
                            nc.sync.dma_start(
                                rows(out[o.number()], q)[:, s * JS:(s + 2) * JS, :],
                                mid[q * C:(q + 1) * C, o.buffer(), s * JS:(s + 2) * JS, :],
                            ).then_inc(stored[o.buffer()][s // 2], 16)

            turns(sp, turn)
            for of_buffer in stored:
                for quarter in of_buffer:
                    sp.wait_ge(quarter, 16 * Q * (N // 2))

        @block.gpsimd
        def _(pool):
            nc.gpsimd.memset(zrow[:, :], 0.0)
            for t in (a_hi, a_lo, b_hi, b_lo, m_hi):
                nc.gpsimd.memset(t[:, :, 0:2], 0.0)
                nc.gpsimd.memset(t[:, :, PITCH - 2:PITCH], 0.0)
            for t in (pairs, beside):
                nc.gpsimd.memset(t[:, :, :, 0:2], 0.0)
                nc.gpsimd.memset(t[:, :, :, PITCH - 3:PITCH], 0.0)
                nc.gpsimd.memset(t[:, 0, 0, 2:PITCH - 3], 0.0)
                nc.gpsimd.memset(t[:, NJ, 1, 2:PITCH - 3], 0.0)
            nc.gpsimd.memset(m_hi[:, 0, 2:2 + W], 0.0)
            nc.gpsimd.memset(m_hi[:, NJ + 1, 2:2 + W], 0.0)
            nc.gpsimd.memset(s5_pair[:, :, :, :], 0.0)
            nc.gpsimd.memset(s5_side[:, :, :, :], 0.0)
            nc.gpsimd.memset(s5_low[:, :, :, :], 0.0).then_inc(zeroed, 1)

            pool.wait_ge(zeroed, 1)
            hi, his, lo = parts5
            pool.wait_ge(w5_bounded, 1)
            nc.gpsimd.tensor_scalar(w5[:, :, :], w5[:, :, :], wfac[:, 1:2], None, ALU.mult).then_inc(w5_split, 1)
            pool.wait_ge(w5_split, 1)
            nc.gpsimd.tensor_copy(hi[:, :, :], w5[:, :, :]).then_inc(w5_split, 1)
            pool.wait_ge(w5_split, 2)
            nc.gpsimd.tensor_scalar(his[:, :, :], hi[:, :, :], 1.0 / LOW, None, ALU.mult).then_inc(w5_split, 1)
            nc.gpsimd.tensor_tensor(lo[:, :, :], w5[:, :, :], hi[:, :, :], ALU.subtract).then_inc(w5_split, 1)
            pool.wait_ge(w5_split, 4)
            copies = [0]

            def place(dst, src):
                nc.gpsimd.tensor_copy(dst, src).then_inc(placed, 1)
                copies[0] += 1
                pool.wait_ge(placed, copies[0])

            def taps(t, part, dy):
                return t[part, :, dy * K5:(dy + 1) * K5].rearrange("p o t -> p t o")

            for kind, q, at, o, dy, side in stationary5():
                part, col = slice(q * C, (q + 1) * C), slice(o * C, (o + 1) * C)
                if kind == "pair":
                    place(s5_pair[part, at, :, col], taps((hi, his)[side], part, dy))
                elif kind == "low":
                    place(s5_low[part, at, :, col], taps(lo, part, dy))
                else:
                    src = lo[part, :, dy * K5 + side:(dy + 1) * K5:2].rearrange("p o t -> p t o")
                    place(s5_side[part, at, 0:DX2 - side, col], src)

            def turn(o):
                for s in range(SLOTS):
                    pool.wait_ge(c2_read, SLOTS * o.number() + s + 1)
                    m = mid[:, o.buffer(), s * JS:(s + 1) * JS, :]
                    nc.gpsimd.tensor_tensor(m, m, conv_out[:, s % BANKS, :, :], ALU.add).then_inc(out_added, 1)

            with pool.Fori(0, N // 2) as k:
                turn(Image(k, 0))
                turn(Image(k, 1))

        @block.scalar
        def _(act):
            def high(which, j, i):
                if which == 1:
                    n = i + 1
                    act.wait_ge(norm1, STEPS1 * n.number() + j + 1)
                    if j < 4:
                        src = x_odd[:, j * RUN:(j + 1) * RUN, :]
                        dst = a_hi[:, j * RUN:(j + 1) * RUN, 2:2 + W]
                    else:
                        src = x_odd[0:C, NJ, :]
                        dst = a_hi[0:C, NJ, 2:2 + W]
                    nc.scalar.activation(dst, src, ACT.Copy, scale=1.0 / LOW).then_inc(hi1, 1)
                    b0, b1 = (j * RUN, (j + 1) * RUN) if j < 4 else (NJ, NJ + 1)
                    if j < 4:
                        nc.scalar.activation(b_hi[0:2 * C, b0:b1, 2:2 + W], x_odd[2 * C:P, b0:b1, :],
                                             ACT.Copy, scale=1.0 / LOW)
                    b0 = max(b0, 1)
                    half = 2 * C if j < 4 else C
                    nc.scalar.activation(b_hi[2 * C:2 * C + half, b0 - 1:b1 - 1, 2:2 + W], x_odd[0:half, b0:b1, :],
                                         ACT.Copy, scale=1.0 / LOW).then_inc(b_set, 1)
                else:
                    act.wait_ge(norm2, STEPS2 * i.number() + j + 1)
                    nc.scalar.activation(m_hi[:, 1 + j * RUN:1 + (j + 1) * RUN, 2:2 + W], norm[:, j % 2, :, :],
                                         ACT.Copy, scale=1.0 / LOW).then_inc(hi2, 1)
                    for t in range(2):
                        last = nc.scalar.activation(beside[2 * C:P, j * RUN + t:(j + 1) * RUN + t, 1 - t, 1:1 + W],
                                                    norm[2 * C * t:2 * C * (t + 1), j % 2, :, :],
                                                    ACT.Copy, scale=1.0 / LOW)
                    last.then_inc(beside2, 1)

            def take_5x5(o, s):
                act.wait_ge(c2_done, SLOTS * o.number() + s + 1)
                if s >= BANKS or not (isinstance(o.k, int) and o.number() == 0):
                    act.wait_ge(out_added, SLOTS * o.number() + s + 1 - BANKS)
                nc.scalar.activation(conv_out[:, s % BANKS, :, :],
                                     psum[:, s % BANKS, :].rearrange("p (j w) -> p j w", j=JS),
                                     ACT.Identity, bias=bias[:, 0:1], scale=unscale[:, 1:2]).then_inc(c2_read, 1)

            def take_root(i, c0, c1):
                act.wait_ge(var_ready, i.number() + 2)
                nc.scalar.activation(root[:, c0:c1], gvar[:, c0:c1], ACT.Sqrt).then_inc(root_ready, 1)

            act.wait_ge(s3_zero, 1)
            act.wait_ge(w3_split, 1)
            for n, t in enumerate(parts3):
                for q in range(Q):
                    for o in range(2):
                        if 0 <= q - o < K3:
                            part = slice(q * C, (q + 1) * C)
                            last_copy = nc.scalar.activation(
                                s3[part, n, :, o * C:(o + 1) * C],
                                t[part, :, (q - o) * K3:(q - o + 1) * K3].rearrange("p o t -> p t o"), ACT.Copy)
            last_copy.then_inc(s3_set, 1)

            def turn(i, first=False, inner=False, last=False, end=False):
                o = i + -1
                steps = plan(i, first, last)
                if is_image(i, 0):
                    take_root(i, 0, 2)
                    behind = {4: 0, 6: 1}
                    for n, (which, j) in enumerate(steps[EARLY - 1]):
                        high(which, j, i)
                        if n in behind:
                            take_5x5(i, behind[n])
                    return
                if is_image(i, 1):
                    high(2, 2, o)
                    take_5x5(o, EARLY - 1)
                    high(2, 3, o)
                elif inner or last or end:
                    for j in left_over(i):
                        high(2, j, o)
                for s in range(EARLY if is_image(i, 1) else 0, SLOTS):
                    if inner or last or end:
                        take_5x5(o, s)
                    if end:
                        continue
                    if s == root_at(i):
                        take_root(i, 1 if last else 0, 1 if first else 2)
                    for which, j in steps.get(s, []):
                        high(which, j, i)

            turns(act, turn)

        @block.vector
        def _(dve):
            nc.vector.memset(ones[:, :], 1.0).then_inc(ones_set, 1)
            nc.vector.memset(s3[:, :, :, :], 0.0).then_inc(s3_zero, 1)
            for t in (b_hi, b_lo):
                nc.vector.memset(t[P - C:P, NJ - 1, 2:2 + W], 0.0)
            steps_w = [0]

            def own_step(ins):
                steps_w[0] += 1
                ins.then_inc(wchain, 1)
                dve.wait_ge(wchain, steps_w[0])

            def stats_in(n, banks):
                for s in banks:
                    nc.vector.bn_stats(bn[:, 0, s, :], x_even[:, n.buffer(), s * JS:(s + 1) * JS, :]).then_inc(bn_x, 1)

            def input_stats(n, banks=range(SLOTS)):
                dve.wait_ge(even_in[n.buffer()], 16 * Q * (n.uses() + 1))
                stats_in(n, banks)

            def split_w3():
                hi, his, lo = parts3
                own_step(nc.vector.tensor_scalar(w3n[:, :, :], w3n[:, :, :], wfac[:, 0:1], None, ALU.mult))
                own_step(nc.vector.tensor_copy(hi[:, :, :], w3n[:, :, :]))
                nc.vector.tensor_scalar(his[:, :, :], hi[:, :, :], 1.0 / LOW, None, ALU.mult)
                nc.vector.tensor_tensor(lo[:, :, :], w3n[:, :, :], hi[:, :, :], ALU.subtract).then_inc(w3_split, 1)

            def largest(w, n):
                nc.vector.tensor_reduce(bound[:, n:n + 1], w[:, :, :].rearrange("p o t -> p (o t)"), AX.X,
                                        ALU.max, apply_absolute_value=True).then_inc(w_bound, 1)

            def power_of_two(n, sums):
                at = slice(n, n + 1)
                dve.wait_ge(w_summed, sums)
                own_step(nc.vector.tensor_scalar(power[:, at], psum[:, B_SETUP + n, 0:1], 2.0 ** -100, None, ALU.max))
                own_step(nc.vector.tensor_scalar(power[:, at].bitcast(U32), power[:, at].bitcast(U32), 0x7F800000, None,
                                                 ALU.bitwise_and))
                own_step(nc.vector.reciprocal(wfac[:, at], power[:, at]))
                own_step(nc.vector.tensor_scalar(wfac[:, at], wfac[:, at], WTOP, None, ALU.mult))
                own_step(nc.vector.tensor_scalar(unscale[:, at], power[:, at], 1.0 / (WTOP * PIX), None, ALU.mult))

            def setup3():
                dve.wait_ge(w3_loaded, 16 * (Q + 1))
                own_step(nc.vector.tensor_reduce(score[:, :], w3[:, :, :].rearrange("p o t -> p t o"), AX.X, ALU.add,
                                                 apply_absolute_value=True))
                own_step(nc.vector.tensor_scalar(small[:, 0:1], thr[:, :], 0.0, None, ALU.max))
                own_step(nc.vector.tensor_scalar(mask[:, :], score[:, :], 1.0 / C, small[:, 0:1], ALU.mult, ALU.subtract))
                own_step(nc.vector.tensor_scalar(mask[:, :], mask[:, :], 0.0, None, ALU.is_gt))
                own_step(nc.vector.tensor_scalar(mask0[:, :], score[:, :], 1.0 / C, 0.0, ALU.mult, ALU.is_gt))
                nc.vector.tensor_reduce(small[:, 1:2], mask[:, :], AX.X, ALU.add).then_inc(kept_counted, 1)
                dve.wait_ge(w_summed, 1)
                own_step(nc.vector.tensor_scalar(small[:, 2:3], psum[:, B_SETUP, 0:1], 1.0 / (Q * C * T3), 0.01,
                                                 ALU.mult, ALU.is_le))
                own_step(nc.vector.scalar_tensor_tensor(mask[:, :], mask0[:, :], small[:, 2:3], mask[:, :], ALU.mult, ALU.max))
                for t in range(T3):
                    ins = nc.vector.tensor_scalar(w3n[:, :, t], w3[:, :, t], mask[:, t:t + 1], None, ALU.mult)
                own_step(ins)
                largest(w3n, 0)
                dve.wait_ge(w_loaded, 16 * (2 * Q + 1))
                largest(w5, 1)
                power_of_two(0, 2)
                power_of_two(1, 3)
                nc.vector.memset(carrier[:, 0:1], 0.0).then_inc(w5_bounded, 1)
                split_w3()

            def normalize(which, j, i):
                if which == 1:
                    if j < 4:
                        v = x_odd[:, j * RUN:(j + 1) * RUN, :]
                        m, s = gmean[:, i.buffer(), 0:1], gscale[:, i.buffer(), 0:1]
                    else:
                        v = x_odd[0:C, NJ, :]
                        m, s = gmean[0:C, i.buffer(), 0:1], gscale[0:C, i.buffer(), 0:1]
                    nc.vector.tensor_scalar(v, v, m, s, ALU.subtract, ALU.mult).then_inc(norm1, 1)
                else:
                    if j >= 2 or not (isinstance(i.k, int) and i.number() == 0):
                        dve.wait_ge(beside2, STEPS2 * i.number() + j - 1)
                    nc.vector.tensor_scalar(norm[:, j % 2, :, :], mid[:, i.buffer(), j * RUN:(j + 1) * RUN, :],
                                            gmean[:, i.buffer(), 1:2], gscale[:, i.buffer(), 1:2], ALU.subtract, ALU.mult).then_inc(norm2, 1)

            def low(which, j, i):
                if which == 1:
                    n = i + 1
                    count = STEPS1 * n.number() + j + 1
                    dve.wait_ge(hi1, count)
                    if j < 4:
                        part, b0, b1 = slice(0, P), j * RUN, (j + 1) * RUN
                    else:
                        part, b0, b1 = slice(0, C), NJ, NJ + 1
                    nc.vector.scalar_tensor_tensor(a_lo[part, b0:b1, 2:2 + W], a_hi[part, b0:b1, 2:2 + W], -LOW,
                                                   x_odd[part, b0:b1, :], ALU.mult, ALU.add).then_inc(lo1, 1)
                    dve.wait_ge(lo1, count)
                    if j < 4:
                        nc.vector.tensor_copy(b_lo[0:2 * C, b0:b1, 2:2 + W], a_lo[2 * C:P, b0:b1, 2:2 + W])
                    first = max(b0, 1)
                    half = 2 * C if j < 4 else C
                    nc.vector.tensor_copy(b_lo[2 * C:2 * C + half, first - 1:b1 - 1, 2:2 + W],
                                          a_lo[0:half, first:b1, 2:2 + W]).then_inc(ready1, 1)
                else:
                    count = STEPS2 * i.number() + j + 1
                    blocks = slice(1 + j * RUN, 1 + (j + 1) * RUN)
                    dve.wait_ge(hi2, count)
                    nc.vector.scalar_tensor_tensor(m_lo[:, j % 2, :, :], m_hi[:, blocks, 2:2 + W],
                                                   -LOW, norm[:, j % 2, :, :], ALU.mult, ALU.add).then_inc(lo2, 1)
                    for t in range(2):
                        at, src = slice(j * RUN + t, (j + 1) * RUN + t), slice(2 * C * t, 2 * C * (t + 1))
                        for dst in (pairs, beside):
                            nc.vector.tensor_copy(dst[0:2 * C, at, 1 - t, 2:2 + W], m_hi[src, blocks, 2:2 + W])
                    dve.wait_ge(lo2, count)
                    for t in range(2):
                        at, src = slice(j * RUN + t, (j + 1) * RUN + t), slice(2 * C * t, 2 * C * (t + 1))
                        last = nc.vector.tensor_copy(pairs[2 * C:P, at, 1 - t, 2:2 + W], m_lo[src, j % 2, :, :])
                    last.then_inc(ready2, 1)

            def left(i, steps):
                for n, j in enumerate(steps):
                    normalize(2, j, i + -1)
                    if n:
                        low(2, steps[n - 1], i + -1)
                low(2, steps[-1], i + -1)

            def turn(i, first=False, inner=False, last=False, end=False):
                if end:
                    left(i, left_over(i))
                    return
                if first:
                    setup3()
                    dve.wait_ge(first_half_in, 16 * Q)
                    stats_in(i + 1, range(SLOTS // 2))
                    input_stats(i + 1, range(SLOTS // 2, SLOTS))
                def stats_mid(s):
                    dve.wait_ge(c1_read, SLOTS * i.number() + s + 1)
                    nc.vector.bn_stats(bn[:, 1, s, :], mid[:, i.buffer(), s * JS:(s + 1) * JS, :]).then_inc(bn_mid, 1)

                if not first:
                    for s in range(SLOTS):
                        if is_image(i, 1) and s in (0, 2):
                            left(i, [left_over(i)[s // 2]])
                        if s % 2 == 0 and not (isinstance(i.k, int) and i.number() < 2):
                            dve.wait_ge(stored[i.buffer()][s // 2], 16 * Q * i.uses())
                        dve.wait_ge(c1_done, SLOTS * i.number() + s + 1)
                        nc.vector.scalar_tensor_tensor(
                            mid[:, i.buffer(), s * JS:(s + 1) * JS, :],
                            psum[:, s % BANKS, :].rearrange("p (j w) -> p j w", j=JS), unscale[:, 0:1],
                            x_even[:, i.buffer(), s * JS:(s + 1) * JS, :], ALU.mult, ALU.add).then_inc(c1_read, 1)
                        if s:
                            stats_mid(s - 1)
                        if is_image(i, 0) or is_image(i, 2):
                            input_stats(i + 1, STATS_BEHIND[i.number()][s])
                    stats_mid(SLOTS - 1)
                if is_image(i, 1):
                    input_stats(i + 1)
                if not last:
                    n = i + 1
                    dve.wait_ge(bn_x, SLOTS * (n.number() + 1))
                    nc.vector.memset(carrier[:, 0:1], 0.0)
                    nc.vector.bn_aggr(mv[:, 0, :], bn[:, 0, :, :].rearrange("p s k -> p (s k)")).then_inc(stat_ready, 1)
                if not first:
                    dve.wait_ge(bn_mid, SLOTS * (i.number() + 1))
                    nc.vector.memset(carrier[:, 1:2], 0.0)
                    nc.vector.bn_aggr(mv[:, 1, :], bn[:, 1, :, :].rearrange("p s k -> p (s k)")).then_inc(stat_ready, 1)
                c0, c1 = (0, 1) if first else (1, 2) if last else (0, 2)
                stage = i.number() + 1
                done = [0]

                def step(ins):
                    done[0] += 1
                    ins.then_inc(gstep, 1)
                    dve.wait_ge(gstep, STEPS_G * stage + done[0])

                dve.wait_ge(stat_ready, 1 if first else 2 * N if last else 2 * i.number() + 3)
                dve.wait_ge(mean_mixed, stage + 1)
                step(nc.vector.tensor_copy(gmean[:, i.buffer(), c0:c1], psum[:, B_MEAN, c0:c1]))
                step(nc.vector.tensor_tensor(spread[:, c0:c1], mv[:, c0:c1, 0], gmean[:, i.buffer(), c0:c1], ALU.subtract))
                step(nc.vector.tensor_tensor(spread[:, c0:c1], spread[:, c0:c1], spread[:, c0:c1], ALU.mult))
                nc.vector.tensor_tensor(spread[:, c0:c1], spread[:, c0:c1], mv[:, c0:c1, 1], ALU.add).then_inc(spread_ready, 1)
                if (inner or last) and not is_image(i, 1):
                    left(i, left_over(i))
                dve.wait_ge(var_mixed, stage + 1)
                nc.vector.tensor_scalar(gvar[:, c0:c1], psum[:, B_VAR, c0:c1], EPS, None, ALU.add).then_inc(var_ready, 1)
                dve.wait_ge(root_ready, stage + 1)
                step(nc.vector.reciprocal(rinv[:, c0:c1], root[:, c0:c1]))
                step(nc.vector.tensor_tensor(newton[:, c0:c1], gvar[:, c0:c1], rinv[:, c0:c1], ALU.mult))
                step(nc.vector.tensor_tensor(newton[:, c0:c1], newton[:, c0:c1], rinv[:, c0:c1], ALU.mult))
                step(nc.vector.tensor_scalar(newton[:, c0:c1], newton[:, c0:c1], -0.5, 1.5, ALU.mult, ALU.add))
                step(nc.vector.scalar_tensor_tensor(gscale[:, i.buffer(), c0:c1], rinv[:, c0:c1], PIX * LOW, newton[:, c0:c1],
                                                    ALU.mult, ALU.mult))
                if first:
                    dve.wait_ge(zeroed, 1)
                if not last:
                    dve.wait_ge(odd_in, 16 * Q * (stage + 1))
                    nc.vector.tensor_scalar(x_odd[0:C, 0, :], zrow[:, :], gmean[0:C, i.buffer(), 0:1], None, ALU.add).then_inc(pad_set, 1)
                    dve.wait_ge(pad_set, stage + 1)
                steps = plan(i, first, last)
                flat = [(s, *t) for s in range(SLOTS) for t in steps.get(s, [])]
                ahead = not (first or is_image(i, 0) or is_image(i, 1) or isinstance(i.k, int) and i.number() > N - 3)
                for n in range(len(flat) + 1):
                    if n < len(flat):
                        normalize(*flat[n][1:], i)
                    if n:
                        low(*flat[n - 1][1:], i)
                    if ahead and n == len(flat) - 2:
                        input_stats(i + 2)

            turns(dve, turn)

        @block.tensor
        def _(pe):
            def over_partitions(bank, src):
                nc.tensor.matmul(psum[:, bank, 0:1], ones[:, :], src, start=True, stop=True).then_inc(w_summed, 1)

            pe.wait_ge(ones_set, 1)
            pe.wait_ge(kept_counted, 1)
            over_partitions(B_SETUP, small[:, 1:2])
            pe.wait_ge(w_bound, 1)
            over_partitions(B_SETUP, bound[:, 0:1])
            pe.wait_ge(w_bound, 2)
            over_partitions(B_SETUP + 1, bound[:, 1:2])
            pe.wait_ge(w_loaded, 16 * (2 * Q + 1))

            def keep_warm(n):
                for _ in range(n):
                    nc.tensor.matmul(psum[:, B_SPARE, 0:P], ones[:, :], ones[:, :], start=True, stop=True)

            def conv3(i, s):
                n = i
                pe.wait_ge(ready1, STEPS1 * n + s // 2 + 1 + s % 2)
                pe.wait_ge(b_set, STEPS1 * n + s // 2 + 1 + s % 2)
                products = [(p, dx) for p in range(3) for dx in range(K3)]
                for m, (p, dx) in enumerate(products):
                    for t in range(2):
                        src = ((a_hi, b_hi), (a_lo, b_lo), (a_hi, b_hi))[p][t]
                        last = nc.tensor.matmul(
                            psum[t * 2 * C:(t + 1) * 2 * C, s % BANKS, :].rearrange("p (j w) -> p j w", j=JS),
                            s3[:, p, dx, :], src[:, s * JS:(s + 1) * JS, 1 + dx:1 + dx + W],
                            start=(m == 0), stop=(m == len(products) - 1))
                last.then_inc(c1_done, 1)

            def conv5(i, s):
                runs = min((s + 1) * JS // RUN + 1, STEPS2)
                pe.wait_ge(ready2, STEPS2 * i + runs)
                pe.wait_ge(beside2, STEPS2 * i + runs)
                products = [("pair", d, dx) for d in range(3) for dx in range(K5)]
                products += [("low", 0, dx) for dx in range(K5)] + [("side", 0, dx) for dx in range(0, K5, 2)]
                for m, (kind, d, dx) in enumerate(products):
                    for t in range(2):
                        if kind == "pair":
                            b, h = divmod(t + d, 2)
                            wt, src = s5_pair[:, d, dx, :], pairs[:, s * JS + b:(s + 1) * JS + b, h, dx:dx + W]
                        elif kind == "low":
                            wt, src = s5_low[:, t, dx, :], m_hi[:, s * JS + 1:(s + 1) * JS + 1, dx:dx + W]
                        else:
                            wt = s5_side[:, t, dx // 2, :]
                            src = beside[:, s * JS + t:(s + 1) * JS + t, t, dx:dx + W]
                        last = nc.tensor.matmul(
                            psum[t * 2 * C:(t + 1) * 2 * C, s % BANKS, :].rearrange("p (j w) -> p j w", j=JS),
                            wt, src, start=(m == 0), stop=(m == len(products) - 1))
                last.then_inc(c2_done, 1)

            def mix_mean(i, c0, c1):
                pe.wait_ge(stat_ready, 2 * N if c0 else 1 if c1 == 1 else 2 * i + 3)
                nc.tensor.matmul(psum[:, B_MEAN, c0:c1], mix[:, :], mv[:, c0:c1, 0], start=True, stop=True).then_inc(mean_mixed, 1)

            def mix_var(i, c0, c1):
                pe.wait_ge(spread_ready, i + 2)
                nc.tensor.matmul(psum[:, B_VAR, c0:c1], mix[:, :], spread[:, c0:c1], start=True, stop=True).then_inc(var_mixed, 1)

            def turn(i, first=False, inner=False, last=False, end=False):
                c0, c1 = (0, 1) if first else (1, 2) if last else (0, 2)
                if not (first or end):
                    for s in range(SLOTS):
                        if s >= BANKS:
                            pe.wait_ge(c1_read, SLOTS * i + s + 1 - BANKS)
                        elif isinstance(i, int) and i == 1:
                            if s < EARLY:
                                pe.wait_ge(c2_read, s + 1)
                            else:
                                pe.wait_ge(c1_read, s + 1 + BANKS)
                        elif inner or last:
                            pe.wait_ge(c2_read, SLOTS * (i - 2) + s + 1 + BANKS)
                        conv3(i, s)
                if first or isinstance(i, int) and i == 0:
                    mix_mean(i, c0, c1)
                    mix_var(i, c0, c1)
                    keep_warm(18)
                if first:
                    return
                if isinstance(i, int) and i == 0:
                    pe.wait_ge(placed, len(stationary5()))
                    for s in range(EARLY):
                        pe.wait_ge(c1_read, s + 1 + BANKS)
                        conv5(0, s)
                    return
                done = EARLY if isinstance(i, int) and i == 1 else 0
                for s in range(done, SLOTS):
                    if s >= done + BANKS:
                        pe.wait_ge(c2_read, SLOTS * (i - 1) + s + 1 - BANKS)
                    elif end:
                        pe.wait_ge(c2_read, SLOTS * (i - 2) + s + 1 + BANKS)
                    else:
                        pe.wait_ge(c1_read, SLOTS * i + s % BANKS + 1 + BANKS)
                    conv5(i - 1, s)
                    if s == mix_at(i) and not end:
                        mix_mean(i, c0, c1)
                    if s == mix_at(i) + 1 and not end:
                        mix_var(i, c0, c1)

            turn(-1, first=True)
            pe.wait_ge(s3_set, 1)
            turn(0)
            turn(1, inner=True)
            with pe.Fori(2, N - 1) as i:
                turn(i, inner=True)
            turn(N - 1, last=True)
            turn(N, end=True)


_INS = ["x", "L0_conv_weight", "L0_conv_threshold", "L1_conv_kernel", "L1_conv_bias"]


def kernel(**inputs):
    import numpy as np
    import concourse.bacc as bacc
    from concourse.bass_utils import run_bass_kernel_spmd as run

    nc = bacc.Bacc("TRN2", target_bir_lowering=False, num_devices=1)
    arrays, args = {}, []
    for name in _INS:
        a = np.ascontiguousarray(inputs[name])
        arrays[name + "_dram"] = a
        args.append(nc.dram_tensor(name + "_dram", a.shape, mybir.dt.from_np(a.dtype), kind="ExternalInput").ap())
    group = (np.arange(P) % C) // GROUP
    mix = (group[:, None] == group[None, :]).astype(np.float32) / (Q * GROUP)
    arrays["mix_dram"] = mix
    args.append(nc.dram_tensor("mix_dram", mix.shape, F32, kind="ExternalInput").ap())
    shape = arrays["x_dram"].shape
    args.append(nc.dram_tensor("out_dram", shape, F32, kind="ExternalOutput").ap())
    two_blocks(nc, *args)
    return run(nc, [arrays], core_ids=[0]).results[0]["out_dram"]
```
